# Optimizing a Trainium2 kernel written in Bass

```python
import numpy as np
import jax
import jax.numpy as jnp

def _softmax(x, axis=-1):
    return jax.nn.softmax(x, axis=axis)

def _gelu(x):
    return jax.nn.gelu(x, approximate=True)

def _silu(x):
    return jax.nn.silu(x)

def _sigmoid(x):
    return jax.nn.sigmoid(x)

def _layernorm(x, axis=-1, eps=1e-05):
    m = jnp.mean(x, axis=axis, keepdims=True)
    v = jnp.var(x, axis=axis, keepdims=True)
    return (x - m) / jnp.sqrt(v + eps)

def _scatter_add(tgt, idx, src, axis=0):
    return tgt.at[idx].add(src)

def _segment_sum(src, seg, n):
    return jax.ops.segment_sum(src, seg, n)
kernel_name = 'mk_seq_postln_d1_jaxref_r4_1e0df5'

def setup_inputs(seed: int=0):
    np.random.seed(seed)
    _w = jnp.asarray

    def _L0_attn_setup():
        import jax, jax.numpy as jnp
        import numpy as np
        B, T, D = (8, 1024, 256)

        def _rg_lru(x, Wi, bi, Wg, bg, Wo, bo):
            u = jnp.einsum('btd,ed->bte', x, Wi) + bi
            g = jax.nn.sigmoid(jnp.einsum('btd,ed->bte', x, Wg) + bg)

            def step(h, gu):
                g_t, u_t = gu
                h = g_t * h + (1.0 - g_t) * u_t
                return (h, h)
            h0 = jnp.zeros((x.shape[0], x.shape[2]), dtype=u.dtype)
            _, h = jax.lax.scan(step, h0, (jnp.swapaxes(g, 0, 1), jnp.swapaxes(u, 0, 1)))
            h = jnp.swapaxes(h, 0, 1)
            return jnp.einsum('btd,ed->bte', h, Wo) + bo
        key = jax.random.key(seed)
        ks = jax.random.split(key, 7)
        s = 1.0 / np.sqrt(D)
        return {'x': jax.random.normal(ks[0], (B, T, D), dtype=jnp.float32), 'Wi': jax.random.uniform(ks[1], (D, D), jnp.float32, -s, s), 'bi': jax.random.uniform(ks[2], (D,), jnp.float32, -s, s), 'Wg': jax.random.uniform(ks[3], (D, D), jnp.float32, -s, s), 'bg': jax.random.uniform(ks[4], (D,), jnp.float32, -s, s), 'Wo': jax.random.uniform(ks[5], (D, D), jnp.float32, -s, s), 'bo': jax.random.uniform(ks[6], (D,), jnp.float32, -s, s)}
    _L0_attn_in = _L0_attn_setup()

    def _L0_ffn_setup():
        import jax, jax.numpy as jnp
        import numpy as np
        B, T, C, D = (2, 1024, 256, 128)
        E = 8
        MIN_E = 2
        EPS = 1e-12
        NEG = -1000000000.0

        def _xavier(key, shape, fan_in, fan_out):
            bound = (6.0 / (fan_in + fan_out)) ** 0.5
            return jax.random.uniform(key, shape, jnp.float32, -bound, bound)

        def _forward(hidden_states, sim_matrix, gates, q_proj, k_proj, v_proj, o_proj):
            b, t, c = hidden_states.shape
            x = hidden_states.reshape(b * t, c)
            xn = x / jnp.maximum(jnp.linalg.norm(x, axis=-1, keepdims=True), EPS)
            sn = sim_matrix / jnp.maximum(jnp.linalg.norm(sim_matrix, axis=0, keepdims=True), EPS)
            logits = xn @ sn - jax.nn.sigmoid(gates)
            gated = jax.nn.relu(logits)
            mask = (gated > 0).astype(logits.dtype)
            inactive = jnp.sum(mask, axis=1) == 0
            top_idx = jax.lax.top_k(logits, MIN_E)[1]
            n = mask.shape[0]
            fb = jnp.zeros_like(mask).at[jnp.arange(n)[:, None], top_idx].set(1.0)
            mask = jnp.where(inactive[:, None] & (fb > 0), 1.0, mask)
            masked_logits = jnp.where(mask > 0, gated, NEG)
            routing_weights = jax.nn.softmax(masked_logits, axis=-1)
            m = jax.lax.stop_gradient(mask)
            q = jnp.einsum('tc,ecd,te->td', x, q_proj, m)
            k = jnp.einsum('tc,ecd,te->td', x, k_proj, m)
            v = jnp.einsum('tc,ecd,te->td', x, v_proj, m)
            qh = q.reshape(b, t, D)
            kh = k.reshape(b, t, D)
            vh = v.reshape(b, t, D)
            scores = jnp.einsum('bqd,bkd->bqk', qh, kh) / jnp.sqrt(jnp.asarray(D, qh.dtype))
            causal = jnp.tril(jnp.ones((t, t), bool))
            scores = jnp.where(causal, scores, jnp.finfo(scores.dtype).min)
            attn = jax.nn.softmax(scores, axis=-1)
            attn_out = jnp.einsum('bqk,bkd->bqd', attn, vh).reshape(b * t, D)
            final = jnp.einsum('td,edc,te->tc', attn_out, o_proj, m * routing_weights)
            return final.reshape(b, t, c)
        key = jax.random.key(seed)
        k = jax.random.split(key, 6)
        hidden_states = jax.random.normal(k[0], (B, T, C), jnp.float32)
        sim_matrix = jax.random.normal(k[1], (C, E), jnp.float32)
        gates = jnp.zeros((E,), jnp.float32)
        q_proj = _xavier(k[2], (E, C, D), C, D)
        k_proj = _xavier(k[3], (E, C, D), C, D)
        v_proj = _xavier(k[4], (E, C, D), C, D)
        o_proj = _xavier(k[5], (E, D, C), D, C)
        return dict(hidden_states=hidden_states, sim_matrix=sim_matrix, gates=gates, q_proj=q_proj, k_proj=k_proj, v_proj=v_proj, o_proj=o_proj)
    _L0_ffn_in = _L0_ffn_setup()
    _d = {'L0_attn_x': _L0_attn_in['x'], 'L0_attn_Wi': _L0_attn_in['Wi'], 'L0_attn_bi': _L0_attn_in['bi'], 'L0_attn_Wg': _L0_attn_in['Wg'], 'L0_attn_bg': _L0_attn_in['bg'], 'L0_attn_Wo': _L0_attn_in['Wo'], 'L0_attn_bo': _L0_attn_in['bo'], 'L0_ffn_sim_matrix': _L0_ffn_in['sim_matrix'], 'L0_ffn_gates': _L0_ffn_in['gates'], 'L0_ffn_q_proj': _L0_ffn_in['q_proj'], 'L0_ffn_k_proj': _L0_ffn_in['k_proj'], 'L0_ffn_v_proj': _L0_ffn_in['v_proj'], 'L0_ffn_o_proj': _L0_ffn_in['o_proj']}
    _x0 = _d['L0_attn_x']
    _d['L0_attn_x'] = jax.random.normal(jax.random.fold_in(jax.random.key(seed), 1), (16, 1024, 256), dtype=_x0.dtype)
    del _x0
    return _d

def reference(L0_attn_x, L0_attn_Wi, L0_attn_bi, L0_attn_Wg, L0_attn_bg, L0_attn_Wo, L0_attn_bo, L0_ffn_sim_matrix, L0_ffn_gates, L0_ffn_q_proj, L0_ffn_k_proj, L0_ffn_v_proj, L0_ffn_o_proj):

    def _L0_attn_ref(x, Wi, bi, Wg, bg, Wo, bo):
        import jax, jax.numpy as jnp
        import numpy as np
        B, T, D = (8, 1024, 256)

        def _rg_lru(x, Wi, bi, Wg, bg, Wo, bo):
            u = jnp.einsum('btd,ed->bte', x, Wi) + bi
            g = jax.nn.sigmoid(jnp.einsum('btd,ed->bte', x, Wg) + bg)

            def step(h, gu):
                g_t, u_t = gu
                h = g_t * h + (1.0 - g_t) * u_t
                return (h, h)
            h0 = jnp.zeros((x.shape[0], x.shape[2]), dtype=u.dtype)
            _, h = jax.lax.scan(step, h0, (jnp.swapaxes(g, 0, 1), jnp.swapaxes(u, 0, 1)))
            h = jnp.swapaxes(h, 0, 1)
            return jnp.einsum('btd,ed->bte', h, Wo) + bo
        return _rg_lru(x, Wi, bi, Wg, bg, Wo, bo)

    def _L0_ffn_ref(hidden_states, sim_matrix, gates, q_proj, k_proj, v_proj, o_proj):
        import jax, jax.numpy as jnp
        import numpy as np
        B, T, C, D = (2, 1024, 256, 128)
        E = 8
        MIN_E = 2
        EPS = 1e-12
        NEG = -1000000000.0

        def _xavier(key, shape, fan_in, fan_out):
            bound = (6.0 / (fan_in + fan_out)) ** 0.5
            return jax.random.uniform(key, shape, jnp.float32, -bound, bound)

        def _forward(hidden_states, sim_matrix, gates, q_proj, k_proj, v_proj, o_proj):
            b, t, c = hidden_states.shape
            x = hidden_states.reshape(b * t, c)
            xn = x / jnp.maximum(jnp.linalg.norm(x, axis=-1, keepdims=True), EPS)
            sn = sim_matrix / jnp.maximum(jnp.linalg.norm(sim_matrix, axis=0, keepdims=True), EPS)
            logits = xn @ sn - jax.nn.sigmoid(gates)
            gated = jax.nn.relu(logits)
            mask = (gated > 0).astype(logits.dtype)
            inactive = jnp.sum(mask, axis=1) == 0
            top_idx = jax.lax.top_k(logits, MIN_E)[1]
            n = mask.shape[0]
            fb = jnp.zeros_like(mask).at[jnp.arange(n)[:, None], top_idx].set(1.0)
            mask = jnp.where(inactive[:, None] & (fb > 0), 1.0, mask)
            masked_logits = jnp.where(mask > 0, gated, NEG)
            routing_weights = jax.nn.softmax(masked_logits, axis=-1)
            m = jax.lax.stop_gradient(mask)
            q = jnp.einsum('tc,ecd,te->td', x, q_proj, m)
            k = jnp.einsum('tc,ecd,te->td', x, k_proj, m)
            v = jnp.einsum('tc,ecd,te->td', x, v_proj, m)
            qh = q.reshape(b, t, D)
            kh = k.reshape(b, t, D)
            vh = v.reshape(b, t, D)
            scores = jnp.einsum('bqd,bkd->bqk', qh, kh) / jnp.sqrt(jnp.asarray(D, qh.dtype))
            causal = jnp.tril(jnp.ones((t, t), bool))
            scores = jnp.where(causal, scores, jnp.finfo(scores.dtype).min)
            attn = jax.nn.softmax(scores, axis=-1)
            attn_out = jnp.einsum('bqk,bkd->bqd', attn, vh).reshape(b * t, D)
            final = jnp.einsum('td,edc,te->tc', attn_out, o_proj, m * routing_weights)
            return final.reshape(b, t, c)
        return _forward(hidden_states, sim_matrix, gates, q_proj, k_proj, v_proj, o_proj)
    x = L0_attn_x
    x = _layernorm(x + _L0_attn_ref(x, L0_attn_Wi, L0_attn_bi, L0_attn_Wg, L0_attn_bg, L0_attn_Wo, L0_attn_bo), axis=-1)
    x = _layernorm(x + _L0_ffn_ref(x, L0_ffn_sim_matrix, L0_ffn_gates, L0_ffn_q_proj, L0_ffn_k_proj, L0_ffn_v_proj, L0_ffn_o_proj), axis=-1)
    return x

_drawn_inputs = setup_inputs


def setup_inputs(seed=0):
    import zlib

    import numpy as np

    out = dict(_drawn_inputs(seed))
    spreads = {'L0_ffn_gates': (0.0, 0.1)}
    factors = {}
    for name, (base, spread) in spreads.items():
        noise = np.random.default_rng([zlib.crc32(name.encode()), seed]).standard_normal(out[name].shape)
        drawn = base * np.exp(spread * noise) if base else spread * noise
        out[name] = jnp.asarray(drawn.astype(out[name].dtype))
    for name, factor in factors.items():
        out[name] = (out[name] * factor).astype(out[name].dtype)
    return out
```

```python
import concourse.bass as bass
import numpy as np
from concourse import mybir
from contextlib import ExitStack

B, T, C = 16, 1024, 256
E, D = 8, 128
P = 128
NT = T // P
HT = T // 2
KC = C // P
UNITS = 2 * E
EPS = 1e-5
NORM_FLOOR = 1e-12
UP = 2.0 ** 8
DOWN = 2.0 ** -8
SCORE = float(D) ** -0.5
OFF = 1e9
CAUSAL = -3.0e38
PREV, THIS, NEXT = -1, 0, 1

XM_RING, MK_RING, TMP_RING = 4, 2, 2


def order():
    first = {
        0: [("x_load", (), NEXT), ("v_turn", (1,), PREV), ("fin", (0,), PREV)],
        1: [("score", (4,), PREV), ("fin_norm", (0,), PREV)],
        2: [("x_turn", (0,), NEXT), ("x_turn", (1,), NEXT)],
        3: [("score", (5,), PREV), ("p_turn", (4, 0), PREV), ("x_turn", (2,), NEXT)],
        4: [("p_turn", (4, 1), PREV)],
        5: [("x_turn", (3,), NEXT), ("gate", (0, 0), NEXT)][:1],
        6: [("score", (6,), PREV), ("p_turn", (5, 0), PREV)],
        7: [("p_turn", (5, 1), PREV), ("gate", (0, 0), NEXT), ("inp", (0, 0), NEXT)],
        8: [("gate", (0, 1), NEXT), ("inp", (0, 1), NEXT)],
        9: [("score", (7,), PREV), ("p_turn", (6, 0), PREV)],
        10: [("p_turn", (6, 1), PREV), ("h_split", (0,), NEXT)],
        11: [("gate", (1, 0), NEXT), ("inp", (1, 0), NEXT)],
        12: [("p_turn", (7, 0), PREV)],
        13: [("p_turn", (7, 1), PREV), ("gate", (1, 1), NEXT), ("inp", (1, 1), NEXT)],
        14: [("pv", (1,), PREV)],
        15: [("h_split", (1,), NEXT), ("weigh", (1,), PREV)],
    }
    second = {
        0: [("v_turn", (0,), THIS), ("x1_sum", (0,), NEXT)],
        1: [("score", (0,), THIS), ("x1_sum", (1,), NEXT), ("fin", (1,), PREV)],
        2: [("score", (1,), THIS), ("x1_sum", (2,), NEXT), ("fin_norm", (1,), PREV)],
        3: [("p_turn", (0, 0), THIS), ("score", (2,), THIS)],
        4: [("x1_sum", (3,), NEXT), ("ln", (), NEXT)],
        5: [("p_turn", (1, 0), THIS), ("score", (3,), THIS), ("ln_apply", (), NEXT)],
        6: [("p_turn", (2, 0), THIS)],
        7: [("x1_turn", (0,), NEXT), ("x1_turn", (1,), NEXT)],
        8: [("x1_turn", (2,), NEXT), ("p_turn", (3, 0), THIS)],
        9: [("x1_turn", (3,), NEXT)],
        10: [("logits", (), NEXT), ("pv", (0,), THIS)],
        11: [("weigh", (0,), THIS), ("route_mask", (), NEXT)],
        12: [("mask_turn", (), NEXT)],
        13: [("route_max", (), NEXT)],
        14: [("route_soft", (), NEXT)],
    }
    for table, start, tiles, who in ((first, 16, range(4, 8), PREV), (second, 12, range(4), THIS)):
        spots = np.linspace(start, 23, 16).astype(int)
        for n, (tile, part) in enumerate((t, p) for t in tiles for p in range(4)):
            table.setdefault(int(spots[n]), []).append(("o_proj", (tile, part), who))
            if part == 3:
                table[int(spots[n])].append(("tile_end", (tile,), who))
    steps = []
    for half, table in ((0, first), (1, second)):
        for slot in range(E):
            u = half * E + slot
            ahead = u + 3
            steps.append(("mask", (ahead % UNITS,), THIS if ahead < UNITS else NEXT))
            for o in range(3):
                steps.append(("qkv", (u, o), THIS))
                if slot == E - 1 and o == 2:
                    steps.append(("qkv_out", (half,), THIS))
                steps += table.get(3 * slot + o, [])
    return steps


ORDER = order()
ITERATIONS = range(-1, B + 1)

def bank_use(name, args):
    if name == "mask":
        return (3,), "full3", ("free3",)
    if name == "score":
        return ((4, 5), "full4", ("free4",)) if args[0] >= 4 else ((4 + args[0] % 2,), f"full{4 + args[0] % 2}", (f"free{4 + args[0] % 2}",))
    if name == "o_proj":
        return ((5,), "full5", ("side_scaled", "side_scaled")) if args[1] % 2 else ((4,), "full4", ("main_added", "main_added"))
    bank = {"x_turn": lambda: 6 + args[0] % 2, "gate": lambda: 7, "inp": lambda: 6,
            "x1_sum": lambda: 6 + args[0] % 2, "x1_turn": lambda: 6 + args[0] % 2, "logits": lambda: 6,
            "mask_turn": lambda: 7, "v_turn": lambda: 7, "p_turn": lambda: 7, "pv": lambda: 6}.get(name)
    if bank is None:
        return None
    return (bank(),), f"full{bank()}", (f"free{bank()}",)


def count_banks():
    count, last, ahead, full, freed = {}, {}, {}, {}, {}
    for it in ITERATIONS:
        for n, (name, args, who) in enumerate(ORDER):
            use = bank_use(name, args)
            if use is None or not 0 <= it + who < B:
                continue
            banks, signal, frees = use
            need = {}
            for k in banks:
                for s, v in last.get(k, {}).items():
                    need[s] = max(need.get(s, 0), v)
            ahead[it, n] = need
            count[signal] = count.get(signal, 0) + 1
            full[it, n] = (signal, count[signal])
            for s in frees:
                count[s] = count.get(s, 0) + 1
            freed[it, n] = {s: count[s] for s in frees}
            for k in banks:
                last[k] = freed[it, n]
    return ahead, full, freed


AHEAD, FULL, FREED = count_banks()
PLACE = {(name, args): (n, who) for n, (name, args, who) in enumerate(ORDER)}
LOOP_FIRST, LOOP_PAIRS = 1, 7


class At:

    def __init__(self, k0, turn=None):
        self.k0, self.turn = k0, turn

    def count(self, of):
        here = of(self.k0)
        if self.turn is None:
            return here
        step = of(self.k0 + 2) - here
        return self.turn * step + here if step else here

    def has(self, who):
        return 0 <= self.k0 + who < B

    def wait(self, eng, sem, of):
        if of(self.k0) > 0:
            eng.wait_ge(sem, self.count(of))


def rglru_moe(nc, x, Wi, bi, Wg, bg, Wo, bo, sim, gates, q_proj, k_proj, v_proj, o_proj, out):
    f32, f32r, f16, bf16 = mybir.dt.float32, mybir.dt.float32r, mybir.dt.float16, mybir.dt.bfloat16
    ALU, ACT, AX = mybir.AluOpType, mybir.ActivationFunctionType, mybir.AxisListType

    ctx = ExitStack()
    with ctx:
        def sb(name, shape, dt):
            return ctx.enter_context(nc.sbuf_tensor(name, shape, dt))

        sems = {}

        def sem(name):
            if name not in sems:
                sems[name] = ctx.enter_context(nc.semaphore(name))
            return sems[name]

        ident = sb("ident", [P, P], f32)
        identb = sb("identb", [P, P], bf16)
        causal = sb("causal", [P, P], bf16)
        earlier = sb("earlier", [P, E, E], f32)
        own_tile = sb("own_tile", [NT * E, NT], bf16)
        pick3 = sb("pick3", [NT * E, E, NT], f32)
        pick1 = sb("pick1", [NT * E, E], f32)
        pick = sb("pick", [NT * E, E, P], bf16)
        halves = sb("halves", [P, 2 * NT], f32)
        wr = sb("wr", [P, 2, 3, KC, C], f32r)
        wqkv = sb("wqkv", [P, 2, 3, E, KC, D], f16)
        wo_e = sb("wo_e", [P, 2, E * C], f32r)
        sn = sb("sn", [P, KC, 2 * E], f16)
        sim_sb = sb("sim_sb", [P, KC, E], f32)
        sim_sq = sb("sim_sq", [P, KC, E], f32)
        sim_n = sb("sim_n", [P, 3, E], f32)
        gate_sb = sb("gate_sb", [P, 3, E], f32)
        bias_i = sb("bias_i", [P, KC], f32)
        bias_g = sb("bias_g", [P, 2, KC], f32)
        bias_o = sb("bias_o", [P, C], f32)
        xin = sb("xin", [P, NT, C], f32)
        xh = sb("xh", [P, 2, KC, HT], f32r)
        xl = sb("xl", [P, 2, KC, HT], f32r)
        gbuf = sb("gbuf", [P, 2, HT], f32)
        vbuf = sb("vbuf", [P, HT], f32)
        hbuf = sb("hbuf", [P, KC, HT], f32)
        x1 = sb("x1", [P, 2, NT, C], f32)
        x1t = sb("x1t", [P, 2, 2 * KC, T], f16)
        st = sb("st", [P, NT, 6], f32)
        mv = sb("mv", [P, NT, 2], f32)
        vp = sb("vp", [P, 2 * NT], f32)
        rs = sb("rs", [P, 2 * NT], f32)
        shift = sb("shift", [P, NT], f32)
        rnorm = sb("rnorm", [P, 3, NT], f32)
        rt = sb("rt", [P, 10, NT, E], f32)
        cmp2 = gbuf[:, :, :].rearrange("p s (t q) -> p s t q", t=NT)
        rv = sb("rv", [P, 5, NT], f32)
        maskb2 = sb("maskb2", [P, 2, NT, E], bf16)
        maskb = maskb2[:, 0, :, :]
        epsilons = sb("epsilons", [P, NT], f32)
        channels = sb("channels", [P, NT], f32)
        gw = sb("gw", [P, 2, NT, E], f32)
        spread = sb("spread", [NT * E, 2, NT, P], bf16)
        mk = sb("mk", [P, MK_RING, HT], f16)
        xm32 = sb("xm32", [P, XM_RING * 2 * KC * HT // 2], f32)
        xm = xm32[:, :].bitcast(f16).rearrange("p (r s t) -> p r s t", r=XM_RING, s=2 * KC)
        qk = sb("qk", [P, 2, 2, T], f32r)
        vt = sb("vt", [P, HT], f32)
        v = sb("v", [P, 2, NT, D], f16)
        p32 = sb("p32", [P, 2, T], f32)
        pt32 = sb("pt32", [P, 2 * NT * HT // 2], f32)
        pt = pt32[:, :].bitcast(f16).rearrange("p (s n t) -> p s n t", s=2, n=NT)
        negmax = sb("negmax", [P, NT], f32)
        scaledmax = sb("scaledmax", [P, NT], f32)
        psums = sb("psums", [P, NT], f32)
        pinv = sb("pinv", [P, NT], f32)
        cw = sb("cw", [P, NT, E], f32)
        a = sb("a", [P, 2, HT], f32r)
        tmp = sb("tmp", [P, TMP_RING, C], f32)
        ones = tmp[:, 0, 0:P]
        side = sb("side", [P, 2, C], f32)
        st2 = sb("st2", [P, NT, 6], f32)
        mv2 = sb("mv2", [P, NT, 2], f32)
        vp2 = sb("vp2", [P, NT], f32)
        rs2 = sb("rs2", [P, NT], f32)
        shift2 = sb("shift2", [P, NT], f32)
        y = sb("y", [P, 4, C], f32)

        w_raw = p32[:, :, :].rearrange("p a t -> p (a t)")[:, 0:3 * KC * C].rearrange(
            "p (w m c) -> p w m c", w=3, m=KC)
        q_raw, k_raw = (xm32[:, n * 2048:(n + 1) * 2048] for n in range(2))
        v_raw, o_raw = (pt32[:, n * 2048:(n + 1) * 2048] for n in range(2))

        banks = [ctx.enter_context(nc.psum_tensor(f"bank{n}", [P, HT], f32)) for n in range(4)]
        wide = ctx.enter_context(nc.psum_tensor("wide", [P, T], f32))
        banks += [wide[:, 0:HT], wide[:, HT:T]]
        banks += [ctx.enter_context(nc.psum_tensor(f"bank{n}", [P, HT], f32)) for n in (6, 7)]
        banks = [b if n in (4, 5) else b[:, :] for n, b in enumerate(banks)]

        x_v = x.rearrange("b (j p) c -> b p j c", p=P)
        out_v = out.rearrange("b (j p) c -> b p j c", p=P)

        def bank_ready(eng, at, job):
            n = PLACE[job][0]
            for s in AHEAD[at.k0, n]:
                at.wait(eng, sem(s), lambda it: AHEAD[it, n][s])

        def bank_full(eng, at, job):
            n = PLACE[job][0]
            at.wait(eng, sem(FULL[at.k0, n][0]), lambda it: FULL[it, n][1])

        def bank_read(eng, at, job, who, part=None):
            n, own = PLACE[job]
            back = who - own
            if (at.k0 + back, n) not in FREED:
                return
            for s in FREED[at.k0 + back, n]:
                at.wait(eng, sem(s), lambda it: FREED[it + back, n][s])

        def full_signal(at, job):
            return sem(FULL[at.k0, PLACE[job][0]][0])

        def batch_wait(eng, at, name, per_batch, k, who):
            at.wait(eng, sem(name), lambda it: per_batch * (it + who) + k)

        def alone(eng):
            eng.wait_ge(sem("consts"), 1)

        def walk(eng, parts):
            def iteration(at):
                for name, args, who in ORDER:
                    if name in parts and at.has(who):
                        parts[name](at, *args)
            for it in range(-1, LOOP_FIRST):
                iteration(At(it))
            with eng.Fori(0, LOOP_PAIRS) as turn:
                iteration(At(LOOP_FIRST, turn))
                iteration(At(LOOP_FIRST + 1, turn))
            for it in range(LOOP_FIRST + 2 * LOOP_PAIRS, B + 1):
                iteration(At(it))

        block = ctx.enter_context(nc.Block())

        @block.sync
        def _(sp):
            sp.sem_inc(sem("y_free"), 16)
            sp.dma_start(xin[:, :, :], x_v[0]).then_inc(sem("x_loaded"), 16)
            for n, w in enumerate((Wi, Wg, Wo)):
                sp.dma_start(w_raw[:, n, :, :], w.rearrange("(m p) c -> p m c", p=P)).then_inc(sem("w_loaded"), 16)
            with nc.allow_non_contiguous_dma(reason="a few hundred values"):
                sp.dma_start(bias_i[:, :], bi.rearrange("(m p) -> p m", p=P)).then_inc(sem("small_loaded"), 16)
                sp.dma_start(bias_g[:, 0, :], bg.rearrange("(m p) -> p m", p=P)).then_inc(sem("small_loaded"), 16)
            sp.dma_start(bias_o[:, :], bo.partition_broadcast(P)).then_inc(sem("small_loaded"), 16)
            sp.dma_start(gate_sb[:, 0, :], gates.partition_broadcast(P)).then_inc(sem("small_loaded"), 16)
            sp.dma_start(sim_sb[:, :, :], sim.rearrange("(k p) e -> p k e", p=P)).then_inc(sem("small_loaded"), 16)
            for raw, w in ((q_raw, q_proj), (k_raw, k_proj), (v_raw, v_proj)):
                sp.dma_start(raw.rearrange("p (e k d) -> p e k d", e=E, k=KC),
                             w.rearrange("e (k p) d -> p e k d", p=P)).then_inc(sem("qkv_loaded"), 16)
            sp.dma_start(o_raw.rearrange("p (e c) -> p e c", e=E),
                         o_proj.rearrange("e d c -> d e c")).then_inc(sem("o_loaded"), 16)

            def x_load(at):
                if at.k0 == -1:
                    return
                batch_wait(sp, at, "x1_ready", NT, 0, NEXT)
                b = at.count(lambda it: it + NEXT)
                src = x_v[b] if at.turn is None else x_v[bass.ds(b, 1)][0]
                sp.dma_start(xin[:, :, :], src).then_inc(sem("x_loaded"), 16)

            def fin_norm(at, c):
                batch_wait(sp, at, "y_ready", 8, 4 * c + 4, PREV)
                b = at.count(lambda it: it + PREV)
                dst = out_v[b] if at.turn is None else out_v[bass.ds(b, 1)][0]
                sp.dma_start(dst[:, 4 * c:4 * c + 4, :], y[:, :, :]).then_inc(sem("y_free"), 16)

            walk(sp, {"x_load": x_load, "fin_norm": fin_norm})
            sp.wait_ge(sem("y_free"), 16 * (2 * B + 1))

        @block.tensor
        def _(pe):
            def passes(dst, pairs, first=True, last=True):
                for n, (w, m) in enumerate(pairs):
                    r = pe.matmul(dst, lhsT=w, rhs=m, start=first and n == 0, stop=last and n == len(pairs) - 1)
                return r

            def split(w, m):
                return [(w(0), m(0)), (w(1), m(0)), (w(0), m(1))]

            pe.wait_ge(sem("consts"), 1)
            pe.wait_ge(sem("w_loaded"), 48)
            for n in range(3):
                for k in range(KC):
                    for m in range(KC):
                        r = pe.transpose(banks[n][:, k * C + m * P:k * C + (m + 1) * P],
                                         w_raw[:, n, m, k * P:(k + 1) * P], ident[:, :])
                r.then_inc(sem("w_turned"), 1)
            pe.wait_ge(sem("sim_squared"), 1)
            for k in range(KC):
                r = pe.matmul(banks[3][:, 0:E], lhsT=ones, rhs=sim_sq[:, k, :], start=k == 0, stop=k == KC - 1)
            r.then_inc(sem("sim_summed"), 1)
            pe.wait_ge(sem("w_split"), 3)
            pe.wait_ge(sem("sim_normed"), 1)
            pe.wait_ge(sem("qkv_split"), 3)
            pe.wait_ge(sem("o_split"), 1)

            def x_turn(at, g):
                h, k = divmod(g, KC)
                batch_wait(pe, at, "x_loaded", 16, 16, NEXT)
                bank_ready(pe, at, ("x_turn", (g,)))
                for j in range(4):
                    r = pe.transpose(banks[6 + g % 2][:, j * P:(j + 1) * P],
                                     xin[:, 4 * h + j, k * P:(k + 1) * P], ident[:, :])
                r.then_inc(full_signal(at, ("x_turn", (g,))), 1)

            def project(at, name, which, h, m):
                for g in (KC * h, KC * h + 1):
                    bank_read(pe, at, ("x_turn", (g,)), NEXT)
                bank_ready(pe, at, (name, (h, m)))
                dst = banks[6 if name == "inp" else 7]
                pairs = [p for k in range(KC) for p in split(
                    lambda s: wr[:, s, which, k, m * P:(m + 1) * P], lambda s: (xh, xl)[s][:, h, k, :])]
                passes(dst, pairs).then_inc(full_signal(at, (name, (h, m))), 1)

            def x1_sum(at, g):
                h = g // 2
                batch_wait(pe, at, "hl_ready", 4, 2 * h + 2, NEXT)
                bank_ready(pe, at, ("x1_sum", (g,)))
                for t in range(2):
                    j = (2 * g + t) % 4
                    pairs = [(xs, w) for k in range(KC) for w, xs in split(
                        lambda s: wr[:, s, 2, k, :], lambda s: (xh, xl)[s][:, h, k, j * P:(j + 1) * P])]
                    r = passes(banks[6 + g % 2][:, t * C:(t + 1) * C], pairs)
                r.then_inc(full_signal(at, ("x1_sum", (g,))), 1)

            def x1_turn(at, g):
                h, k = divmod(g, KC)
                par = (at.k0 + NEXT) % 2
                batch_wait(pe, at, "x1_ready", NT, 4 * h + 4, NEXT)
                bank_ready(pe, at, ("x1_turn", (g,)))
                for j in range(4):
                    r = pe.transpose(banks[6 + g % 2][:, j * P:(j + 1) * P],
                                     x1[:, par, 4 * h + j, k * P:(k + 1) * P], ident[:, :])
                r.then_inc(full_signal(at, ("x1_turn", (g,))), 1)

            def logits(at):
                par = (at.k0 + NEXT) % 2
                for g in range(4):
                    bank_read(pe, at, ("x1_turn", (g,)), NEXT)
                bank_ready(pe, at, ("logits", ()))
                for j in range(NT):
                    dst = banks[6][:, j * 2 * E:(j + 1) * 2 * E]
                    tok = slice(j * P, (j + 1) * P)
                    for n, (s, k) in enumerate(((0, 0), (0, 1), (1, 0), (1, 1))):
                        w = 2 * E if s == 0 else E
                        r = pe.matmul(dst[:, 0:w], lhsT=x1t[:, par, s * KC + k, tok], rhs=sn[:, k, 0:w],
                                      start=n == 0, stop=n == 3)
                r.then_inc(full_signal(at, ("logits", ())), 1)

            def mask_turn(at):
                batch_wait(pe, at, "mask_ready", 1, 1, NEXT)
                bank_ready(pe, at, ("mask_turn", ()))
                pe.transpose(banks[7].bitcast(bf16)[:, 0:P], maskb2[:, :, :, :].rearrange("p s t e -> p (s t e)"),
                             identb[:, :]).then_inc(full_signal(at, ("mask_turn", ())), 1)

            def mask(at, u):
                h, e = divmod(u, E)
                who = PLACE["mask", (u,)][1]
                par = (at.k0 + who) % 2
                bank_read(pe, at, ("mask_turn", ()), who)
                bank_ready(pe, at, ("mask", (u,)))
                pe.matmul(banks[3], lhsT=pick[:, e, :], rhs=spread[:, par, 4 * h:4 * h + 4, :].rearrange("p j t -> p (j t)"),
                          start=True, stop=True).then_inc(full_signal(at, ("mask", (u,))), 1)

            def qkv(at, u, o):
                h, e = divmod(u, E)
                slot = u % XM_RING
                if o == 0:
                    batch_wait(pe, at, "xm_ready", UNITS, u + 1, THIS)
                if e == 0:
                    if o < 2:
                        batch_wait(pe, at, "qk_split", 4, 2 * h - 1 + o, THIS)
                    else:
                        batch_wait(pe, at, "vt_ready", 2, h, THIS)
                pairs = [p for k in range(KC) for p in split(
                    lambda s: wqkv[:, s, o, e, k, :], lambda s: xm[:, slot, s * KC + k, :])]
                r = passes(banks[o], pairs, first=e == 0, last=e == E - 1)
                if e == E - 1:
                    r.then_inc(sem("acc_full"), 1)
                elif o == 2:
                    r.then_inc(sem("xm_used"), 1)

            def v_turn(at, h):
                who = PLACE["v_turn", (h,)][1]
                batch_wait(pe, at, "vt_ready", 2, h + 1, who)
                bank_ready(pe, at, ("v_turn", (h,)))
                for j in range(4):
                    r = pe.transpose(banks[7][:, j * P:(j + 1) * P], vt[:, j * P:(j + 1) * P], ident[:, :])
                r.then_inc(full_signal(at, ("v_turn", (h,))), 1)

            def score(at, j):
                who = PLACE["score", (j,)][1]
                c, w = j // 4, (j + 1) * P
                batch_wait(pe, at, "qk_split", 4, 2 * c + 2, who)
                bank_ready(pe, at, ("score", (j,)))
                for lo in range(0, w, HT):
                    hi = min(w, lo + HT)
                    dst = wide[:, lo:hi] if c else banks[4 + j % 2][:, lo:hi]
                    pairs = split(lambda s: qk[:, s, 0, j * P:(j + 1) * P], lambda s: qk[:, s, 1, lo:hi])
                    diag = hi == w
                    passes(dst, pairs, last=not diag)
                    if diag:
                        r = pe.matmul(dst[:, hi - lo - P:hi - lo], lhsT=identb[:, :], rhs=causal[:, :], start=False, stop=True)
                r.then_inc(full_signal(at, ("score", (j,))), 1)

            def p_turn(at, j, part):
                who = PLACE["p_turn", (j, part)][1]
                bank_read(pe, at, ("score", (j,)), who)
                bank_ready(pe, at, ("p_turn", (j, part)))
                for n, kt in enumerate(range(4 * part, min(4 * part + 4, j + 1))):
                    r = pe.transpose(banks[7][:, n * P:(n + 1) * P], p32[:, j % 2, kt * P:(kt + 1) * P], ident[:, :])
                r.then_inc(full_signal(at, ("p_turn", (j, part))), 1)

            def pv(at, c):
                who = PLACE["pv", (c,)][1]
                bank_read(pe, at, ("p_turn", (4 * c + 3, c)), who)
                bank_read(pe, at, ("v_turn", (c,)), who)
                bank_ready(pe, at, ("pv", (c,)))
                tiles = 4 * c + 4
                for kt in range(tiles):
                    q0 = max(0, kt - 4 * c) * P
                    pairs = split(lambda s: v[:, s, kt, :], lambda s: pt[:, s, kt, q0:HT])
                    r = passes(banks[6][:, q0:HT], pairs, first=kt == 0, last=kt == tiles - 1)
                r.then_inc(full_signal(at, ("pv", (c,))), 1)

            def o_proj_part(at, j, part):
                who = PLACE["o_proj", (j, part)][1]
                bank_read(pe, at, ("pv", (j // 4,)), who)
                bank_ready(pe, at, ("o_proj", (j, part)))
                tok = slice((j % 4) * P, (j % 4 + 1) * P)
                pairs = [(at_, w) for w, at_ in split(
                    lambda s: wo_e[:, s, part * 2 * C:(part + 1) * 2 * C], lambda s: a[:, s, tok])]
                passes(banks[4 + part % 2], pairs).then_inc(full_signal(at, ("o_proj", (j, part))), 1)

            walk(pe, {
                "x_turn": x_turn, "gate": lambda at, h, m: project(at, "gate", 1, h, m),
                "inp": lambda at, h, m: project(at, "inp", 0, h, m), "x1_sum": x1_sum, "x1_turn": x1_turn,
                "logits": logits, "mask_turn": mask_turn, "mask": mask, "qkv": qkv, "v_turn": v_turn,
                "score": score, "p_turn": p_turn, "pv": pv, "o_proj": o_proj_part})

        @block.scalar
        def _(act):
            for n in range(3):
                act.wait_ge(sem("w_turned"), n + 1)
                act.activation(wr[:, 0, n, :, :].rearrange("p k c -> p (k c)"), banks[n], ACT.Copy).then_inc(sem("w_high"), 1)
            act.wait_ge(sem("small_loaded"), 80)
            act.activation(bias_g[:, 1, :], bias_g[:, 0, :], ACT.Copy, scale=0.5).then_inc(sem("bias_halved"), 1)
            act.activation(gate_sb[:, 1, :], gate_sb[:, 0, :], ACT.Tanh, scale=0.5).then_inc(sem("gates_tanh"), 1)
            act.wait_ge(sem("qkv_loaded"), 48)
            for o, raw in enumerate((q_raw, k_raw, v_raw)):
                act.activation(wqkv[:, 0, o, :, :, :].rearrange("p e k d -> p (e k d)"), raw, ACT.Copy,
                               scale=UP).then_inc(sem("qkv_high"), 1)
            act.wait_ge(sem("o_loaded"), 16)
            act.activation(wo_e[:, 0, :], o_raw, ACT.Copy).then_inc(sem("o_high"), 1)
            act.wait_ge(sem("bias_halved"), 1)

            def x_turn(at, g):
                h, k = divmod(g, KC)
                bank_read(act, at, ("x1_sum", (2 * h + 1,)), THIS)
                bank_full(act, at, ("x_turn", (g,)))
                act.activation(xh[:, h, k, :], banks[6 + g % 2], ACT.Copy).then_inc(sem("xh_ready"), 1)

            def gate(at, h, m):
                n = 2 * h + m
                batch_wait(act, at, "scanned", 4, n - 1, NEXT)
                bank_full(act, at, ("gate", (h, m)))
                act.activation(gbuf[:, m, :], banks[7], ACT.Tanh, bias=bias_g[:, 1, m:m + 1],
                               scale=0.5).then_inc(sem("free7"), 1)

            def h_split(at, h):
                for m in range(KC):
                    batch_wait(act, at, "scanned", 4, 2 * h + 2, NEXT)
                    act.activation(xh[:, h, m, :], hbuf[:, m, :], ACT.Copy).then_inc(sem("hh_ready"), 1)

            def ln_apply(at):
                par = (at.k0 + NEXT) % 2
                batch_wait(act, at, "ln_shift", 1, 1, NEXT)
                batch_wait(act, at, "y_ready", 8, 8, PREV)
                for j in range(NT):
                    act.activation(x1[:, par, j, :], xin[:, j, :], ACT.Identity, bias=shift[:, j:j + 1],
                                   scale=rs[:, j:j + 1]).then_inc(sem("x1_ready"), 1)

            def x1_turn(at, g):
                h, k = divmod(g, KC)
                par = (at.k0 + NEXT) % 2
                bank_full(act, at, ("x1_turn", (g,)))
                act.activation(x1t[:, par, k, h * HT:(h + 1) * HT], banks[6 + g % 2], ACT.Copy).then_inc(sem("x1h_ready"), 1)

            def route_soft(at):
                batch_wait(act, at, "route_shifted", 1, 1, NEXT)
                act.activation(rt[:, 6, :, :], rt[:, 5, :, :], ACT.Exp).then_inc(sem("route_exp"), 1)

            def mask(at, u):
                who = PLACE["mask", (u,)][1]
                batch_wait(act, at, "xm_ready", UNITS, u - MK_RING + 1, who)
                bank_full(act, at, ("mask", (u,)))
                act.activation(mk[:, u % MK_RING, :], banks[3], ACT.Copy).then_inc(sem("free3"), 1)

            def qkv_out(at, h):
                tok = slice(h * HT, (h + 1) * HT)
                for o in range(2):
                    batch_wait(act, at, "acc_full", 6, 3 * h + o + 1, THIS)
                    bank_read(act, at, ("score", (7,)), PREV)
                    act.activation(qk[:, 0, o, tok], banks[o], ACT.Copy, scale=DOWN).then_inc(sem("qk_high"), 1)
                batch_wait(act, at, "acc_full", 6, 3 * h + 3, THIS)
                act.activation(vt[:, :], banks[2], ACT.Copy, scale=DOWN).then_inc(sem("vt_ready"), 1)

            def v_turn(at, h):
                bank_full(act, at, ("v_turn", (h,)))
                who = PLACE["v_turn", (h,)][1]
                bank_read(act, at, ("pv", (1,)), who - 1)
                act.activation(v[:, 0, 4 * h:4 * h + 4, :].rearrange("p n d -> p (n d)"), banks[7],
                               ACT.Copy).then_inc(sem("vh_ready"), 1)

            def score(at, j):
                who = PLACE["score", (j,)][1]
                w = (j + 1) * P
                if j >= 2:
                    bank_read(act, at, ("p_turn", (j - 2, (j - 2) // 4)), who)
                batch_wait(act, at, "max_scaled", NT, j + 1, who)
                src = wide[:, 0:w] if j >= 4 else banks[4 + j % 2][:, 0:w]
                act.activation(p32[:, j % 2, 0:w], src, ACT.Exp, bias=scaledmax[:, j:j + 1], scale=SCORE,
                               accum_out=psums[:, j:j + 1]).then_inc(sem(bank_use("score", (j,))[2][0]), 1)

            def p_turn(at, j, part):
                who = PLACE["p_turn", (j, part)][1]
                n = min(4, j + 1 - 4 * part)
                c = j // 4
                bank_read(act, at, ("pv", (1 - c,)), who if c else who - 1)
                bank_full(act, at, ("p_turn", (j, part)))
                act.activation(pt[:, 0, 4 * part:4 * part + n, (j % 4) * P:(j % 4 + 1) * P],
                               banks[7][:, 0:n * P].rearrange("p (n q) -> p n q", n=n), ACT.Copy).then_inc(sem("pth_ready"), 1)

            def pv(at, c):
                who = PLACE["pv", (c,)][1]
                bank_read(act, at, ("o_proj", (3 if c else 7, 3)), who if c else who - 1)
                bank_full(act, at, ("pv", (c,)))
                act.activation(a[:, 0, :], banks[6], ACT.Copy).then_inc(sem("ah_ready"), 1)

            def o_proj_part(at, j, part):
                if part % 2 == 0:
                    return
                who = PLACE["o_proj", (j, part)][1]
                batch_wait(act, at, "weighed", 2, j // 4 + 1, who)
                bank_full(act, at, ("o_proj", (j, part)))
                for i in range(2):
                    n = 3 * j + part - 2 + i
                    if part == 1 and i == 0:
                        dst = side[:, j % 2, :]
                        batch_wait(act, at, "tile_summed", NT, j - 1, who)
                    else:
                        dst = tmp[:, n % TMP_RING, :]
                        batch_wait(act, at, "side_added", 3 * NT, n - TMP_RING + 1, who)
                    act.activation(dst, banks[5][:, i * C:(i + 1) * C], ACT.Copy,
                                   scale=cw[:, j, 2 * part + i:2 * part + i + 1]).then_inc(sem("side_scaled"), 1)

            def fin_norm(at, c):
                batch_wait(act, at, "fin_shift", 2, c + 1, PREV)
                batch_wait(act, at, "y_free", 2 * 16, 16 * (c + 1), PREV)
                par = (at.k0 + PREV) % 2
                for n in range(4):
                    j = 4 * c + n
                    act.activation(y[:, n, :], x1[:, par, j, :], ACT.Identity, bias=shift2[:, j:j + 1],
                                   scale=rs2[:, j:j + 1]).then_inc(sem("y_ready"), 1)

            walk(act, {"x_turn": x_turn, "gate": gate, "h_split": h_split, "ln_apply": ln_apply, "x1_turn": x1_turn,
                       "route_soft": route_soft, "mask": mask, "qkv_out": qkv_out, "v_turn": v_turn, "score": score,
                       "p_turn": p_turn, "pv": pv, "o_proj": o_proj_part, "fin_norm": fin_norm})

        @block.vector
        def _(dve):
            dve.wait_ge(sem("small_loaded"), 80)
            dve.tensor_tensor(sim_sq[:, :, :], sim_sb[:, :, :], sim_sb[:, :, :], ALU.mult).then_inc(sem("sim_squared"), 1)
            for n in range(3):
                dve.wait_ge(sem("w_high"), n + 1)
                dve.tensor_tensor(wr[:, 1, n, :, :].rearrange("p k c -> p (k c)"), banks[n],
                                  wr[:, 0, n, :, :].rearrange("p k c -> p (k c)").bitcast(f32),
                                  ALU.subtract).then_inc(sem("w_split"), 1)
            dve.wait_ge(sem("sim_summed"), 1)
            dve.tensor_copy(sim_n[:, 0, :], banks[3][:, 0:E]).then_inc(sem("sim_sum_copied"), 1)
            dve.wait_ge(sem("sim_rooted"), 1)
            dve.tensor_scalar(sim_n[:, 2, :], sim_n[:, 1, :], NORM_FLOOR, DOWN, ALU.max, ALU.mult).then_inc(sem("prep"), 1)
            dve.wait_ge(sem("prep"), 1)
            dve.reciprocal(sim_n[:, 0, :], sim_n[:, 2, :]).then_inc(sem("prep"), 1)
            dve.wait_ge(sem("prep"), 2)
            dve.tensor_tensor(sim_sq[:, :, :], sim_sb[:, :, :], sim_n[:, 0, :].unsqueeze(1).to_broadcast([P, KC, E]),
                              ALU.mult).then_inc(sem("prep"), 1)
            dve.wait_ge(sem("prep"), 3)
            dve.tensor_copy(sn[:, :, 0:E], sim_sq[:, :, :]).then_inc(sem("prep"), 1)
            dve.wait_ge(sem("prep"), 4)
            dve.tensor_tensor(sn[:, :, E:2 * E], sim_sq[:, :, :], sn[:, :, 0:E], ALU.subtract).then_inc(sem("sim_normed"), 1)
            dve.wait_ge(sem("gates_tanh"), 1)
            dve.tensor_scalar(gate_sb[:, 2, :], gate_sb[:, 1, :], 0.5, 0.5, ALU.mult, ALU.add).then_inc(sem("prep"), 1)
            for o, raw in enumerate((q_raw, k_raw, v_raw)):
                dve.wait_ge(sem("qkv_high"), o + 1)
                dve.scalar_tensor_tensor(wqkv[:, 1, o, :, :, :].rearrange("p e k d -> p (e k d)"), raw, UP,
                                         wqkv[:, 0, o, :, :, :].rearrange("p e k d -> p (e k d)"),
                                         ALU.mult, ALU.subtract).then_inc(sem("qkv_split"), 1)
            dve.wait_ge(sem("o_high"), 1)
            dve.tensor_tensor(wo_e[:, 1, :], o_raw, wo_e[:, 0, :].bitcast(f32), ALU.subtract).then_inc(sem("o_split"), 1)
            dve.wait_ge(sem("prep"), 5)
            dve.wait_ge(sem("masks_made"), 3)
            dve.reduce_sum(pick1[:, :], pick3[:, :, :], AX.X).then_inc(sem("prep"), 1)
            dve.wait_ge(sem("prep"), 6)
            dve.tensor_copy(pick[:, :, :], pick1[:, :].unsqueeze(2).to_broadcast([NT * E, E, P])).then_inc(sem("prep"), 1)

            def x_turn(at, g):
                h, k = divmod(g, KC)
                batch_wait(dve, at, "xh_ready", 4, g + 1, NEXT)
                dve.tensor_tensor(xl[:, h, k, :], banks[6 + g % 2], xh[:, h, k, :].bitcast(f32),
                                  ALU.subtract).then_inc(sem(f"free{6 + g % 2}"), 1)

            def inp(at, h, m):
                n = 2 * h + m
                bank_read(dve, at, ("gate", (h, m)), NEXT)
                batch_wait(dve, at, "scanned", 4, n, NEXT)
                dve.tensor_scalar(vbuf[:, :], gbuf[:, m, :], -0.5, 0.5, ALU.mult, ALU.add).then_inc(sem("gates_out"), 1)
                batch_wait(dve, at, "gates_out", 8, 2 * n + 1, NEXT)
                dve.tensor_scalar(gbuf[:, m, :], gbuf[:, m, :], 0.5, 0.5, ALU.mult, ALU.add).then_inc(sem("gates_out"), 1)
                bank_full(dve, at, ("inp", (h, m)))
                dve.scalar_tensor_tensor(vbuf[:, :], banks[6], bias_i[:, m:m + 1], vbuf[:, :],
                                         ALU.add, ALU.mult).then_inc(sem("free6"), 1)
                batch_wait(dve, at, "gates_out", 8, 2 * n + 2, NEXT)
                bank_read(dve, at, ("inp", (h, m)), NEXT)
                if h:
                    batch_wait(dve, at, "hh_ready", 4, 2, NEXT)
                    batch_wait(dve, at, "scanned", 4, m + 1, NEXT)
                else:
                    batch_wait(dve, at, "hh_ready", 4, 0, NEXT)
                dve.tensor_tensor_scan(hbuf[:, m, :], gbuf[:, m, :], vbuf[:, :],
                                       hbuf[:, m, HT - 1:HT] if h else 0.0, ALU.mult, ALU.add).then_inc(sem("scanned"), 1)

            def h_split(at, h):
                for m in range(KC):
                    batch_wait(dve, at, "hh_ready", 4, 2 * h + m + 1, NEXT)
                    dve.tensor_tensor(xl[:, h, m, :], hbuf[:, m, :], xh[:, h, m, :].bitcast(f32),
                                      ALU.subtract).then_inc(sem("hl_ready"), 1)

            def x1_sum(at, g):
                bank_full(dve, at, ("x1_sum", (g,)))
                batch_wait(dve, at, "xb_ready", 1, 1, NEXT)
                two = xin[:, 2 * g:2 * g + 2, :].rearrange("p j c -> p (j c)")
                dve.tensor_tensor(two, banks[6 + g % 2], two, ALU.add).then_inc(sem(f"free{6 + g % 2}"), 1)
                bank_read(dve, at, ("x1_sum", (g,)), NEXT)
                for j in (2 * g, 2 * g + 1):
                    dve.bn_stats(st[:, j, :], xin[:, j, :]).then_inc(sem("ln_partial"), 1)

            def ln(at):
                alone(dve)
                batch_wait(dve, at, "ln_partial", NT, NT, NEXT)
                for j in range(NT):
                    r = dve.bn_aggr(mv[:, j, :], st[:, j, :])
                r.then_inc(sem("ln_stats"), 1)

            def ln_apply(at):
                batch_wait(dve, at, "ln_rstd", 1, 1, NEXT)
                dve.scalar_tensor_tensor(shift[:, :], mv[:, :, 0], -1.0, rs[:, 0:NT], ALU.mult, ALU.mult).then_inc(sem("ln_shift"), 1)
                dve.tensor_tensor(rnorm[:, 0, :], rs[:, NT:2 * NT], rs[:, 0:NT], ALU.mult).then_inc(sem("norm_step"), 1)
                batch_wait(dve, at, "norm_step", 3, 1, NEXT)
                dve.tensor_scalar(rnorm[:, 1, :], rnorm[:, 0, :], NORM_FLOOR, UP, ALU.max, ALU.mult).then_inc(sem("norm_step"), 1)
                batch_wait(dve, at, "norm_step", 3, 2, NEXT)
                dve.reciprocal(rnorm[:, 2, :], rnorm[:, 1, :]).then_inc(sem("norm_step"), 1)

            def x1_turn(at, g):
                h, k = divmod(g, KC)
                par = (at.k0 + NEXT) % 2
                tok = slice(h * HT, (h + 1) * HT)
                batch_wait(dve, at, "x1h_ready", 4, g + 1, NEXT)
                dve.tensor_tensor(x1t[:, par, KC + k, tok], banks[6 + g % 2], x1t[:, par, k, tok],
                                  ALU.subtract).then_inc(sem(f"free{6 + g % 2}"), 1)

            def logits(at):
                bank_full(dve, at, ("logits", ()))
                dve.reduce_sum(rt[:, 7, :, :], banks[6][:, 0:NT * 2 * E].rearrange("p (t s e) -> p t e s", t=NT, s=2),
                               AX.X).then_inc(sem("free6"), 1)

            STEPS = 15
            per_tile = [P, NT, E]
            logit, gated, active, fb, rank, masked, ex = (rt[:, n, :, :] for n in (0, 1, 2, 3, 4, 5, 6))

            def stepper(at, first):
                n = [first]

                def step(r):
                    r.then_inc(sem("route_step"), 1)
                    n[0] += 1
                    k = n[0]
                    batch_wait(dve, at, "route_step", STEPS, k, NEXT)
                return step

            def route_mask(at):
                step = stepper(at, 0)
                batch_wait(dve, at, "norm_step", 3, 3, NEXT)
                bank_read(dve, at, ("logits", ()), NEXT)
                step(dve.tensor_tensor(rt[:, 8, :, :], rt[:, 7, :, :], rnorm[:, 2, :].unsqueeze(2).to_broadcast(per_tile), ALU.mult))
                step(dve.tensor_tensor(logit, rt[:, 8, :, :], gate_sb[:, 2, :].unsqueeze(1).to_broadcast(per_tile), ALU.subtract))
                step(dve.tensor_scalar(active, logit, 0.0, None, ALU.is_gt))
                step(dve.reduce_max(rv[:, 0, :], active, AX.X))
                quad = [P, NT, E, E]
                above = cmp2[:, 0, :, :].rearrange("p t (e j) -> p t e j", e=E)
                equal = cmp2[:, 1, :, :].rearrange("p t (e j) -> p t e j", e=E)
                theirs, mine = logit.unsqueeze(2).to_broadcast(quad), logit.unsqueeze(3).to_broadcast(quad)
                step(dve.tensor_tensor(above, theirs, mine, ALU.is_gt))
                step(dve.tensor_tensor(equal, theirs, mine, ALU.is_equal))
                step(dve.tensor_tensor(equal, equal, earlier[:, :, :].unsqueeze(1).to_broadcast(quad), ALU.mult))
                step(dve.tensor_tensor(above, above, equal, ALU.add))
                step(dve.reduce_sum(rank, above, AX.X))
                step(dve.tensor_scalar(rv[:, 1, :], rv[:, 0, :], -1.0, 1.0, ALU.mult, ALU.add))
                step(dve.scalar_tensor_tensor(fb, rank, 2.0, rv[:, 1, :].unsqueeze(2).to_broadcast(per_tile), ALU.is_lt, ALU.mult))
                dve.tensor_tensor(maskb, active, fb, ALU.max).then_inc(sem("mask_ready"), 1)

            def mask_turn(at):
                par = (at.k0 + NEXT) % 2
                bank_full(dve, at, ("mask_turn", ()))
                src = banks[7].bitcast(bf16)[0:NT * E, 0:P].unsqueeze(1).to_broadcast([NT * E, NT, P])
                dve.tensor_tensor(spread[:, par, :, :], src, own_tile[:, :].unsqueeze(2).to_broadcast([NT * E, NT, P]),
                                  ALU.mult).then_inc(sem("free7"), 1)

            def route_max(at):
                step = stepper(at, 11)
                batch_wait(dve, at, "mask_ready", 1, 1, NEXT)
                step(dve.tensor_scalar(gated, logit, 0.0, None, ALU.max))
                step(dve.tensor_scalar(rt[:, 9, :, :], maskb, OFF, -OFF, ALU.mult, ALU.add))
                step(dve.tensor_tensor(rt[:, 7, :, :], rt[:, 9, :, :], gated, ALU.add))
                step(dve.reduce_max(rv[:, 2, :], rt[:, 7, :, :], AX.X))
                dve.tensor_tensor(masked, rt[:, 7, :, :], rv[:, 2, :].unsqueeze(2).to_broadcast(per_tile),
                                  ALU.subtract).then_inc(sem("route_shifted"), 1)

            def route_soft(at):
                par = (at.k0 + NEXT) % 2
                batch_wait(dve, at, "route_exp", 1, 1, NEXT)
                dve.reduce_sum(rv[:, 3, :], ex, AX.X).then_inc(sem("soft_step"), 1)
                batch_wait(dve, at, "soft_step", 3, 1, NEXT)
                dve.reciprocal(rv[:, 4, :], rv[:, 3, :]).then_inc(sem("soft_step"), 1)
                batch_wait(dve, at, "soft_step", 3, 2, NEXT)
                dve.tensor_tensor(rt[:, 8, :, :], ex, rv[:, 4, :].unsqueeze(2).to_broadcast(per_tile),
                                  ALU.mult).then_inc(sem("soft_step"), 1)
                batch_wait(dve, at, "soft_step", 3, 3, NEXT)
                dve.tensor_tensor(gw[:, par, :, :], rt[:, 8, :, :], maskb, ALU.mult).then_inc(sem("gw_ready"), 1)

            def mask(at, u):
                h, e = divmod(u, E)
                who = PLACE["mask", (u,)][1]
                par = (at.k0 + who) % 2
                bank_read(dve, at, ("mask", (u,)), who)
                old = u - XM_RING
                if old % E == E - 1:
                    batch_wait(dve, at, "acc_full", 6, 3 * (old // E) + 3, who)
                else:
                    done = lambda k: k // E * (E - 1) + k % E + 1
                    batch_wait(dve, at, "xm_used", 2 * (E - 1), done(old), who)
                dve.tensor_tensor(xm[:, u % XM_RING, :, :], x1t[:, par, :, h * HT:(h + 1) * HT],
                                  mk[:, u % MK_RING, :].unsqueeze(1).to_broadcast([P, 2 * KC, HT]),
                                  ALU.mult).then_inc(sem("xm_ready"), 1)

            def qkv_out(at, h):
                tok = slice(h * HT, (h + 1) * HT)
                for o in range(2):
                    batch_wait(dve, at, "qk_high", 4, 2 * h + o + 1, THIS)
                    dve.scalar_tensor_tensor(qk[:, 1, o, tok], banks[o], DOWN, qk[:, 0, o, tok].bitcast(f32),
                                             ALU.mult, ALU.subtract).then_inc(sem("qk_split"), 1)

            def v_turn(at, h):
                who = PLACE["v_turn", (h,)][1]
                batch_wait(dve, at, "vh_ready", 2, h + 1, who)
                dve.tensor_tensor(v[:, 1, 4 * h:4 * h + 4, :].rearrange("p n d -> p (n d)"), banks[7],
                                  v[:, 0, 4 * h:4 * h + 4, :].rearrange("p n d -> p (n d)"), ALU.subtract).then_inc(sem("free7"), 1)

            def score(at, j):
                who = PLACE["score", (j,)][1]
                w = (j + 1) * P
                bank_full(dve, at, ("score", (j,)))
                src = wide[:, 0:w] if j >= 4 else banks[4 + j % 2][:, 0:w]
                dve.reduce_max(negmax[:, j:j + 1], src, AX.X, negate=True).then_inc(sem("max_found"), 1)
                batch_wait(dve, at, "max_found", NT, j + 1, who)
                dve.tensor_scalar(scaledmax[:, j:j + 1], negmax[:, j:j + 1], SCORE, None, ALU.mult).then_inc(sem("max_scaled"), 1)

            def p_turn(at, j, part):
                who = PLACE["p_turn", (j, part)][1]
                n = min(4, j + 1 - 4 * part)
                k = j + 1 if j < 4 else 4 + 2 * (j - 4) + part + 1
                batch_wait(dve, at, "pth_ready", 12, k, who)
                dst = (slice(None), slice(4 * part, 4 * part + n), slice((j % 4) * P, (j % 4 + 1) * P))
                dve.tensor_tensor(pt[:, 1, dst[1], dst[2]], banks[7][:, 0:n * P].rearrange("p (n q) -> p n q", n=n),
                                  pt[:, 0, dst[1], dst[2]], ALU.subtract).then_inc(sem("free7"), 1)

            def pv(at, c):
                who = PLACE["pv", (c,)][1]
                batch_wait(dve, at, "ah_ready", 2, c + 1, who)
                dve.tensor_tensor(a[:, 1, :], banks[6], a[:, 0, :].bitcast(f32), ALU.subtract).then_inc(sem("free6"), 1)

            def weigh(at, c):
                who = PLACE["weigh", (c,)][1]
                par = (at.k0 + who) % 2
                t4 = slice(4 * c, 4 * c + 4)
                bank_read(dve, at, ("score", (4 * c + 3,)), who)
                batch_wait(dve, at, "gw_ready", 1, 1, who)
                dve.reciprocal(pinv[:, t4], psums[:, t4]).then_inc(sem("sum_inverted"), 1)
                batch_wait(dve, at, "sum_inverted", 2, c + 1, who)
                dve.tensor_tensor(cw[:, t4, :], gw[:, par, t4, :], pinv[:, t4].unsqueeze(2).to_broadcast([P, 4, E]),
                                  ALU.mult).then_inc(sem("weighed"), 1)

            def o_proj_part(at, j, part):
                if part % 2:
                    return
                who = PLACE["o_proj", (j, part)][1]
                par = (at.k0 + who) % 2
                batch_wait(dve, at, "weighed", 2, j // 4 + 1, who)
                bank_full(dve, at, ("o_proj", (j, part)))
                for i in range(2):
                    batch_wait(dve, at, "main_added", 4 * NT, 4 * j + part + i, who)
                    dve.scalar_tensor_tensor(x1[:, par, j, :], banks[4][:, i * C:(i + 1) * C],
                                             cw[:, j, 2 * part + i:2 * part + i + 1], x1[:, par, j, :],
                                             ALU.mult, ALU.add).then_inc(sem("main_added"), 1)

            def tile_end(at, j):
                who = PLACE["tile_end", (j,)][1]
                par = (at.k0 + who) % 2
                batch_wait(dve, at, "main_added", 4 * NT, 4 * j + 4, who)
                batch_wait(dve, at, "side_added", 3 * NT, 3 * j + 3, who)
                dve.tensor_tensor(x1[:, par, j, :], x1[:, par, j, :], side[:, j % 2, :], ALU.add).then_inc(sem("tile_summed"), 1)
                batch_wait(dve, at, "tile_summed", NT, j + 1, who)
                dve.bn_stats(st2[:, j, :], x1[:, par, j, :]).then_inc(sem("fin_partial"), 1)
                alone(dve)
                batch_wait(dve, at, "fin_partial", NT, j + 1, who)
                dve.bn_aggr(mv2[:, j, :], st2[:, j, :]).then_inc(sem("fin_stats"), 1)

            def fin_norm(at, c):
                t4 = slice(4 * c, 4 * c + 4)
                batch_wait(dve, at, "fin_rstd", 2, c + 1, PREV)
                dve.scalar_tensor_tensor(shift2[:, t4], mv2[:, t4, 0], -1.0, rs2[:, t4], ALU.mult,
                                         ALU.mult).then_inc(sem("fin_shift"), 1)

            walk(dve, {"x_turn": x_turn, "inp": inp, "h_split": h_split, "x1_sum": x1_sum, "ln": ln, "ln_apply": ln_apply,
                       "x1_turn": x1_turn, "logits": logits, "route_mask": route_mask, "mask_turn": mask_turn, "route_max": route_max,
                       "route_soft": route_soft, "mask": mask, "qkv_out": qkv_out, "v_turn": v_turn, "score": score,
                       "p_turn": p_turn, "pv": pv, "weigh": weigh, "o_proj": o_proj_part, "tile_end": tile_end,
                       "fin_norm": fin_norm})

        @block.gpsimd
        def _(pool):
            pool.memset(ident[:, :], 0.0).then_inc(sem("cleared"), 1)
            pool.memset(causal[:, :], 0.0).then_inc(sem("cleared"), 1)
            pool.memset(earlier[:, :, :], 1.0).then_inc(sem("cleared"), 1)
            pool.memset(pick3[:, :, :], 0.0).then_inc(sem("cleared"), 1)
            pool.memset(own_tile[:, :], 1.0).then_inc(sem("cleared"), 1)
            pool.memset(halves[:, 0:NT], -0.5).then_inc(sem("cleared"), 1)
            pool.memset(halves[:, NT:2 * NT], 0.5).then_inc(sem("cleared"), 1)
            pool.memset(ones, 1.0).then_inc(sem("cleared"), 1)
            pool.memset(epsilons[:, :], EPS).then_inc(sem("cleared"), 1)
            pool.memset(channels[:, :], float(C)).then_inc(sem("cleared"), 1)
            pool.memset(maskb2[:, 1, :, :], 0.0).then_inc(sem("cleared"), 1)
            pool.wait_ge(sem("cleared"), 11)
            pool.affine_select(out=ident[:, :], in_=ident[:, :], compare_op=ALU.not_equal, fill=1.0, base=0,
                               pattern=[[-1, P]], channel_multiplier=1).then_inc(sem("selected"), 1)
            pool.wait_ge(sem("selected"), 1)
            pool.tensor_copy(identb[:, :], ident[:, :]).then_inc(sem("consts"), 1)
            pool.affine_select(out=causal[:, :], in_=causal[:, :], compare_op=ALU.is_ge, fill=CAUSAL, base=0,
                               pattern=[[-1, P]], channel_multiplier=1).then_inc(sem("selected"), 1)
            pool.affine_select(out=earlier[:, :, :], in_=earlier[:, :, :], compare_op=ALU.is_gt, fill=0.0, base=0,
                               pattern=[[1, E], [-1, E]], channel_multiplier=0).then_inc(sem("masks_made"), 1)
            pool.affine_select(out=pick3[:, :, :], in_=pick3[:, :, :], compare_op=ALU.not_equal, fill=1.0, base=0,
                               pattern=[[-1, E], [-E, NT]], channel_multiplier=1).then_inc(sem("masks_made"), 1)
            pool.affine_select(out=own_tile[:, :], in_=own_tile[:, :], compare_op=ALU.is_ge, fill=0.0, base=0,
                               pattern=[[-E, NT]], channel_multiplier=1).then_inc(sem("selected"), 1)
            pool.wait_ge(sem("selected"), 3)
            pool.affine_select(out=own_tile[:, :], in_=own_tile[:, :], compare_op=ALU.is_ge, fill=0.0, base=E - 1,
                               pattern=[[E, NT]], channel_multiplier=-1).then_inc(sem("masks_made"), 1)
            pool.wait_ge(sem("sim_sum_copied"), 1)
            pool.tensor_tensor(sim_n[:, 1, :], sim_n[:, 0, :], halves[:, NT:NT + E], ALU.pow).then_inc(sem("sim_rooted"), 1)
            pool.wait_ge(sem("small_loaded"), 80)

            def x_turn(at, g):
                if g < 3:
                    return
                for k in range(4):
                    bank_full(pool, at, ("x_turn", (k,)))
                pool.tensor_tensor(xin[:, :, :], xin[:, :, :], bias_o[:, :].unsqueeze(1).to_broadcast([P, NT, C]),
                                   ALU.add).then_inc(sem("xb_ready"), 1)

            def ln(at):
                batch_wait(pool, at, "ln_stats", 1, 1, NEXT)
                pool.tensor_tensor(vp[:, 0:NT], mv[:, :, 1], epsilons[:, :], ALU.add).then_inc(sem("ln_var"), 1)
                pool.tensor_tensor(vp[:, NT:2 * NT], mv[:, :, 1], channels[:, :], ALU.mult).then_inc(sem("ln_var"), 1)
                batch_wait(pool, at, "ln_var", 2, 2, NEXT)
                pool.tensor_tensor(rs[:, :], vp[:, :], halves[:, :], ALU.pow).then_inc(sem("ln_rstd"), 1)

            def o_proj_part(at, j, part):
                if part % 2 == 0:
                    return
                who = PLACE["o_proj", (j, part)][1]
                for i in range(part == 1, 2):
                    n = 3 * j + part - 2 + i
                    batch_wait(pool, at, "side_scaled", 4 * NT, 4 * j + part + i, who)
                    if n % 3:
                        batch_wait(pool, at, "side_added", 3 * NT, n, who)
                    pool.tensor_tensor(side[:, j % 2, :], side[:, j % 2, :], tmp[:, n % TMP_RING, :],
                                       ALU.add).then_inc(sem("side_added"), 1)

            def fin(at, c):
                t4 = slice(4 * c, 4 * c + 4)
                batch_wait(pool, at, "fin_stats", NT, 4 * c + 4, PREV)
                pool.tensor_tensor(vp2[:, t4], mv2[:, t4, 1], epsilons[:, t4], ALU.add).then_inc(sem("fin_var"), 1)
                batch_wait(pool, at, "fin_var", 2, c + 1, PREV)
                pool.tensor_tensor(rs2[:, t4], vp2[:, t4], halves[:, 0:4], ALU.pow).then_inc(sem("fin_rstd"), 1)

            walk(pool, {"x_turn": x_turn, "ln": ln, "o_proj": o_proj_part, "fin": fin})


_INS = ["L0_attn_x", "L0_attn_Wi", "L0_attn_bi", "L0_attn_Wg", "L0_attn_bg", "L0_attn_Wo", "L0_attn_bo",
        "L0_ffn_sim_matrix", "L0_ffn_gates", "L0_ffn_q_proj", "L0_ffn_k_proj", "L0_ffn_v_proj", "L0_ffn_o_proj"]
_OUTS = [((B, T, C), "float32")]


def kernel(**inputs):
    import concourse.bacc as _bacc
    from concourse.bass_utils import run_bass_kernel_spmd as _run

    nc = _bacc.Bacc("TRN2", target_bir_lowering=False, num_devices=1)
    arrays, args = {}, []
    for name in _INS:
        arr = np.ascontiguousarray(inputs[name])
        arrays[f"in_{name}_dram"] = arr
        args.append(nc.dram_tensor(f"in_{name}_dram", arr.shape, mybir.dt.from_np(arr.dtype), kind="ExternalInput").ap())
    for i, (shape, dtype) in enumerate(_OUTS):
        args.append(nc.dram_tensor(f"out_{i}_dram", shape, mybir.dt.from_np(np.dtype(dtype)), kind="ExternalOutput").ap())
    rglru_moe(nc, *args)
    r = _run(nc, [arrays], core_ids=[0])
    return r.results[0]["out_0_dram"]
```

```python
import concourse.bass as bass
import numpy as np
from concourse import mybir
from contextlib import ExitStack

B, T, C = 16, 1024, 256
E, D = 8, 128
P = 128
NT = T // P
HT = T // 2
KC = C // P
UNITS = 2 * E
EPS = 1e-5
NORM_FLOOR = 1e-12
UP = 2.0 ** 8
DOWN = 2.0 ** -8
QK_SCALE = (DOWN * float(D) ** -0.5, DOWN)
OFF = 1e9
CAUSAL = -3.0e38
PREV, THIS, NEXT = -1, 0, 1
FIRST = "first"

XM_RING, MK_RING, TMP_RING = 4, 2, 2


def order():
    gaps = {
        0: [("x_load", (), NEXT), ("v_turn", (1,), PREV), ("score", (4,), PREV)],
        1: [("x_turn", (0,), NEXT), ("fin", (0,), PREV)],
        2: [("exp", (4,), PREV), ("x_turn", (1,), NEXT)],
        3: [("score", (5,), PREV), ("x_turn", (2,), NEXT)],
        4: [("x_turn", (3,), NEXT), ("exp", (5,), PREV), ("fin_norm", (0,), PREV)],
        5: [("p_turn", (4, 0), PREV), ("gate", (0, 0), NEXT), ("w_high", (0,), FIRST)],
        6: [("p_turn", (4, 1), PREV), ("score", (6,), PREV), ("inp", (0, 0), NEXT)],
        7: [("gate", (0, 1), NEXT), ("exp", (6,), PREV)],
        8: [("p_turn", (5, 0), PREV), ("inp", (0, 1), NEXT), ("w_high", (1,), FIRST)],
        9: [("p_turn", (5, 1), PREV), ("score", (7,), PREV), ("h_split", (0,), NEXT), ("gate", (1, 0), NEXT)],
        10: [("inp", (1, 0), NEXT), ("exp", (7,), PREV)],
        11: [("p_turn", (6, 0), PREV), ("gate", (1, 1), NEXT), ("w_high", (2,), FIRST)],
        12: [("p_turn", (6, 1), PREV), ("inp", (1, 1), NEXT)],
        13: [("p_turn", (7, 0), PREV), ("w_high", (3,), FIRST)],
        14: [("p_turn", (7, 1), PREV), ("h_split", (1,), NEXT)],
        16: [("pv", (1,), PREV), ("weigh", (1,), PREV)],
        18: [("x1_sum", (0,), NEXT)],
        19: [("x1_sum", (1,), NEXT)],
        20: [("x1_sum", (2,), NEXT)],
        21: [("x1_sum", (3,), NEXT)],
        23: [("ln", (), NEXT), ("w_low", (0,), FIRST)],
        25: [("score", (0,), THIS), ("ln_apply", (0,), NEXT)],
        26: [("v_turn", (0,), THIS), ("score", (1,), THIS), ("exp", (0,), THIS), ("ln_apply", (1,), NEXT)],
        27: [("exp", (1,), THIS), ("ln_apply", (2,), NEXT)],
        28: [("p_turn", (0, 0), THIS), ("score", (2,), THIS), ("x1_turn", (0,), NEXT), ("w_low", (1,), FIRST)],
        29: [("p_turn", (1, 0), THIS), ("score", (3,), THIS), ("exp", (2,), THIS), ("x1_turn", (1,), NEXT)],
        30: [("exp", (3,), THIS), ("ln_apply", (3,), NEXT), ("fin", (1,), PREV)],
        31: [("p_turn", (2, 0), THIS), ("x1_turn", (2,), NEXT)],
        32: [("p_turn", (3, 0), THIS), ("x1_turn", (3,), NEXT)],
        33: [("logits", (), NEXT), ("fin_norm", (1,), PREV)],
        34: [("pv", (0,), THIS), ("weigh", (0,), THIS), ("route_mask", (), NEXT), ("w_low", (2,), FIRST)],
        38: [("mask_turn", (), NEXT), ("route_max", (), NEXT)],
        40: [("route_soft", (), NEXT)],
        42: [("w_low", (3,), FIRST)],
    }
    for start, end, tiles, who in ((17.5, 25.5, range(4, 8), PREV), (36, 48, range(4), THIS)):
        for n, (tile, part) in enumerate((t, p) for t in tiles for p in range(4)):
            at = start + (end - start) * n / 16
            gaps.setdefault(int(at), []).append(("o_proj", (tile, part), who))
            if part == 3:
                gap, late = (int(at) + 2) % 48, int(at) + 2 >= 48
                gaps.setdefault(gap, []).insert(0, ("tile_end", (tile,), who - late))
    steps = []
    for u in range(UNITS):
        half, slot = divmod(u, E)
        ahead = u + 2
        steps.append(("mask", (ahead % UNITS,), THIS if ahead < UNITS else NEXT))
        for o in range(3):
            steps.append(("qkv", (u, o), THIS))
            if slot == E - 1:
                steps.append(("qkv_out", (half, o), THIS))
            steps += gaps.get(3 * u + o, [])
    return steps


ORDER = order()
ITERATIONS = range(-1, B + 1)

def bank_use(name, args):
    if name == "mask":
        return (3,), "full3", ("free3",)
    if name == "score":
        return ((4, 5), "full4", ("free4",)) if args[0] >= 4 else ((4 + args[0] % 2,), f"full{4 + args[0] % 2}", (f"free{4 + args[0] % 2}",))
    if name == "o_proj":
        if args[1] % 2:
            return (7,), "full7", ("side_scaled", "side_scaled")
        return (4 + args[1] // 2,), f"full{4 + args[1] // 2}", ("main_added", "main_added")
    if name == "x_turn":
        return (6 + args[0] % 2,), f"full{6 + args[0] % 2}", (f"free{6 + args[0] % 2}",)
    bank = { "gate": 6, "inp": 6, "x1_sum": 6, "x1_turn": 6, "logits": 6, "pv": 6, "mask_turn": 6,
            "v_turn": 7, "p_turn": 7}.get(name)
    return bank and ((bank,), f"full{bank}", (f"free{bank}",))


def count_banks():
    count, last, ahead, full, freed = {}, {}, {}, {}, {}
    for it in ITERATIONS:
        for n, (name, args, who) in enumerate(ORDER):
            use = bank_use(name, args)
            if use is None or who == FIRST or not 0 <= it + who < B:
                continue
            banks, signal, frees = use
            need = {}
            for k in banks:
                for s, v in last.get(k, {}).items():
                    need[s] = max(need.get(s, 0), v)
            ahead[it, n] = need
            count[signal] = count.get(signal, 0) + 1
            full[it, n] = (signal, count[signal])
            for s in frees:
                count[s] = count.get(s, 0) + 1
            freed[it, n] = {s: count[s] for s in frees}
            for k in banks:
                last[k] = freed[it, n]
    return ahead, full, freed


AHEAD, FULL, FREED = count_banks()
PLACE = {(name, args): (n, who) for n, (name, args, who) in enumerate(ORDER)}
LOOP_FIRST, LOOP_PAIRS = 1, 7


class At:

    def __init__(self, k0, turn=None):
        self.k0, self.turn = k0, turn

    def count(self, of):
        here = of(self.k0)
        if self.turn is None:
            return here
        step = of(self.k0 + 2) - here
        return self.turn * step + here if step else here

    def has(self, who):
        return self.k0 == -1 if who == FIRST else 0 <= self.k0 + who < B

    def wait(self, eng, sem, of):
        if of(self.k0) > 0:
            eng.wait_ge(sem, self.count(of))


def rglru_moe(nc, x, Wi, bi, Wg, bg, Wo, bo, sim, gates, q_proj, k_proj, v_proj, o_proj, out):
    f32, f32r, f16, bf16 = mybir.dt.float32, mybir.dt.float32r, mybir.dt.float16, mybir.dt.bfloat16
    ALU, ACT, AX = mybir.AluOpType, mybir.ActivationFunctionType, mybir.AxisListType

    ctx = ExitStack()
    with ctx:
        def sb(name, shape, dt):
            return ctx.enter_context(nc.sbuf_tensor(name, shape, dt))

        sems = {}

        def sem(name):
            if name not in sems:
                sems[name] = ctx.enter_context(nc.semaphore(name))
            return sems[name]

        ident = sb("ident", [P, P], f32)
        identb = sb("identb", [P, P], bf16)
        causal = sb("causal", [P, P], bf16)
        earlier = sb("earlier", [P, E, E], f32)
        own_tile = sb("own_tile", [NT * E, NT], bf16)
        pick3 = sb("pick3", [NT * E, E, NT], f32)
        pick1 = sb("pick1", [NT * E, E], f32)
        pick = sb("pick", [NT * E, E, P], bf16)
        halves = sb("halves", [P, 2 * NT], f32)
        wr = sb("wr", [P, 2, 3, KC, C], f32r)
        wqkv = sb("wqkv", [P, 2, 3, E, KC, D], f16)
        wo_e = sb("wo_e", [P, 2, E * C], f32r)
        sn = sb("sn", [P, KC, 2 * E], f16)
        sim_sb = sb("sim_sb", [P, KC, E], f32)
        sim_sq = sb("sim_sq", [P, KC, E], f32)
        sim_n = sb("sim_n", [P, 3, E], f32)
        gate_sb = sb("gate_sb", [P, 3, E], f32)
        bias_i = sb("bias_i", [P, KC], f32)
        bias_g = sb("bias_g", [P, 2, KC], f32)
        bias_o = sb("bias_o", [P, C], f32)
        xin = sb("xin", [P, NT, C], f32)
        xh = sb("xh", [P, 2, KC, HT], f32r)
        xl = sb("xl", [P, 2, KC, HT], f32r)
        gbuf = sb("gbuf", [P, 2, HT], f32)
        vbuf = sb("vbuf", [P, HT], f32)
        hbuf = sb("hbuf", [P, KC, HT], f32)
        x1 = sb("x1", [P, 2, NT, C], f32)
        x1t = sb("x1t", [P, 2, 2 * KC, T], f16)
        st = sb("st", [P, NT, 6], f32)
        mv = sb("mv", [P, NT, 2], f32)
        vp = sb("vp", [P, 2 * NT], f32)
        rs = sb("rs", [P, 2 * NT], f32)
        shift = sb("shift", [P, NT], f32)
        rnorm = sb("rnorm", [P, 3, NT], f32)
        rt = sb("rt", [P, 10, NT, E], f32)
        cmp2 = gbuf[:, :, :].rearrange("p s (t q) -> p s t q", t=NT)
        rv = sb("rv", [P, 5, NT], f32)
        maskb2 = sb("maskb2", [P, 2, NT, E], bf16)
        maskb = maskb2[:, 0, :, :]
        epsilons = sb("epsilons", [P, NT], f32)
        channels = sb("channels", [P, NT], f32)
        gw = sb("gw", [P, 2, NT, E], f32)
        spread = sb("spread", [NT * E, 2, NT, P], bf16)
        mk = sb("mk", [P, MK_RING, HT], f16)
        xm32 = sb("xm32", [P, XM_RING * 2 * KC * HT // 2], f32)
        xm = xm32[:, :].bitcast(f16).rearrange("p (r s t) -> p r s t", r=XM_RING, s=2 * KC)
        qk = sb("qk", [P, 2, 2, T], f32r)
        vt = sb("vt", [P, HT], f32)
        v = sb("v", [P, 2, NT, D], f16)
        p32 = sb("p32", [P, 2, T], f32)
        pt32 = sb("pt32", [P, 2 * NT * HT // 2], f32)
        pt = pt32[:, :].bitcast(f16).rearrange("p (s n t) -> p s n t", s=2, n=NT)
        negmax = sb("negmax", [P, NT], f32)
        psums = sb("psums", [P, NT], f32)
        pinv = sb("pinv", [P, NT], f32)
        cw = sb("cw", [P, NT, E], f32)
        a = sb("a", [P, 2, HT], f32r)
        tmp = sb("tmp", [P, TMP_RING, C], f32)
        ones = tmp[:, 0, 0:P]
        side = sb("side", [P, 2, C], f32)
        st2 = sb("st2", [P, NT, 6], f32)
        mv2 = sb("mv2", [P, NT, 2], f32)
        vp2 = sb("vp2", [P, NT], f32)
        rs2 = sb("rs2", [P, NT], f32)
        shift2 = sb("shift2", [P, NT], f32)
        y = sb("y", [P, 4, C], f32)

        w_raw = p32[:, :, :].rearrange("p a t -> p (a t)")[:, 0:3 * KC * C].rearrange(
            "p (w m c) -> p w m c", w=3, m=KC)
        q_raw, k_raw = (xm32[:, n * 2048:(n + 1) * 2048] for n in range(2))
        v_raw, o_raw = (pt32[:, n * 2048:(n + 1) * 2048] for n in range(2))

        banks = [ctx.enter_context(nc.psum_tensor(f"bank{n}", [P, HT], f32)) for n in range(4)]
        wide = ctx.enter_context(nc.psum_tensor("wide", [P, T], f32))
        banks += [wide[:, 0:HT], wide[:, HT:T]]
        banks += [ctx.enter_context(nc.psum_tensor(f"bank{n}", [P, HT], f32)) for n in (6, 7)]
        banks = [b if n in (4, 5) else b[:, :] for n, b in enumerate(banks)]

        x_v = x.rearrange("b (j p) c -> b p j c", p=P)
        out_v = out.rearrange("b (j p) c -> b p j c", p=P)

        def bank_ready(eng, at, job):
            n = PLACE[job][0]
            for s in AHEAD[at.k0, n]:
                at.wait(eng, sem(s), lambda it: AHEAD[it, n][s])

        def bank_full(eng, at, job, who=None):
            n, own = PLACE[job]
            back = 0 if who is None else who - own
            at.wait(eng, sem(FULL[at.k0 + back, n][0]), lambda it: FULL[it + back, n][1])

        def bank_read(eng, at, job, who):
            n, own = PLACE[job]
            back = who - own
            if (at.k0 + back, n) not in FREED:
                return
            for s in FREED[at.k0 + back, n]:
                at.wait(eng, sem(s), lambda it: FREED[it + back, n][s])

        def full_signal(at, job):
            return sem(FULL[at.k0, PLACE[job][0]][0])

        def batch_wait(eng, at, name, per_batch, k, who):
            at.wait(eng, sem(name), lambda it: per_batch * (it + who) + k)

        def alone(eng):
            eng.wait_ge(sem("consts"), 1)

        def walk(eng, parts):
            def iteration(at):
                for name, args, who in ORDER:
                    if name in parts and at.has(who):
                        parts[name](at, *args)
            for it in range(-1, LOOP_FIRST):
                iteration(At(it))
            with eng.Fori(0, LOOP_PAIRS) as turn:
                iteration(At(LOOP_FIRST, turn))
                iteration(At(LOOP_FIRST + 1, turn))
            for it in range(LOOP_FIRST + 2 * LOOP_PAIRS, B + 1):
                iteration(At(it))

        block = ctx.enter_context(nc.Block())

        @block.sync
        def _(sp):
            sp.sem_inc(sem("y_free"), 16)
            sp.dma_start(xin[:, :, :], x_v[0]).then_inc(sem("x_loaded"), 16)
            for n, w in enumerate((Wi, Wg, Wo)):
                sp.dma_start(w_raw[:, n, :, :], w.rearrange("(m p) c -> p m c", p=P)).then_inc(sem("w_loaded"), 16)
            with nc.allow_non_contiguous_dma(reason="a few hundred values"):
                sp.dma_start(bias_i[:, :], bi.rearrange("(m p) -> p m", p=P)).then_inc(sem("small_loaded"), 16)
                sp.dma_start(bias_g[:, 0, :], bg.rearrange("(m p) -> p m", p=P)).then_inc(sem("small_loaded"), 16)
            sp.dma_start(bias_o[:, :], bo.partition_broadcast(P)).then_inc(sem("small_loaded"), 16)
            sp.dma_start(gate_sb[:, 0, :], gates.partition_broadcast(P)).then_inc(sem("small_loaded"), 16)
            sp.dma_start(sim_sb[:, :, :], sim.rearrange("(k p) e -> p k e", p=P)).then_inc(sem("small_loaded"), 16)
            for raw, w in ((q_raw, q_proj), (k_raw, k_proj), (v_raw, v_proj)):
                sp.dma_start(raw.rearrange("p (e k d) -> p e k d", e=E, k=KC),
                             w.rearrange("e (k p) d -> p e k d", p=P)).then_inc(sem("qkv_loaded"), 16)
            sp.dma_start(o_raw.rearrange("p (e c) -> p e c", e=E),
                         o_proj.rearrange("e d c -> d e c")).then_inc(sem("o_loaded"), 16)

            def x_load(at):
                if at.k0 == -1:
                    return
                batch_wait(sp, at, "x1_ready", NT, 0, NEXT)
                b = at.count(lambda it: it + NEXT)
                src = x_v[b] if at.turn is None else x_v[bass.ds(b, 1)][0]
                sp.dma_start(xin[:, :, :], src).then_inc(sem("x_loaded"), 16)

            def fin_norm(at, c):
                batch_wait(sp, at, "y_ready", 8, 4 * c + 4, PREV)
                b = at.count(lambda it: it + PREV)
                dst = out_v[b] if at.turn is None else out_v[bass.ds(b, 1)][0]
                sp.dma_start(dst[:, 4 * c:4 * c + 4, :], y[:, :, :]).then_inc(sem("y_free"), 16)

            walk(sp, {"x_load": x_load, "fin_norm": fin_norm})
            sp.wait_ge(sem("y_free"), 16 * (2 * B + 1))

        @block.tensor
        def _(pe):
            def passes(dst, pairs, first=True, last=True):
                for n, (w, m) in enumerate(pairs):
                    r = pe.matmul(dst, lhsT=w, rhs=m, start=first and n == 0, stop=last and n == len(pairs) - 1)
                return r

            def split(w, m):
                return [(w(0), m(0)), (w(1), m(0)), (w(0), m(1))]

            pe.wait_ge(sem("consts"), 1)
            pe.wait_ge(sem("w_loaded"), 48)
            for n in range(3):
                for k in range(KC):
                    for m in range(KC):
                        r = pe.transpose(banks[n][:, k * C + m * P:k * C + (m + 1) * P],
                                         w_raw[:, n, m, k * P:(k + 1) * P], ident[:, :])
                r.then_inc(sem("w_turned"), 1)
            pe.wait_ge(sem("sim_squared"), 1)
            for k in range(KC):
                r = pe.matmul(banks[3][:, 0:E], lhsT=ones, rhs=sim_sq[:, k, :], start=k == 0, stop=k == KC - 1)
            r.then_inc(sem("sim_summed"), 1)

            def x_turn(at, g):
                h, k = divmod(g, KC)
                batch_wait(pe, at, "x_loaded", 16, 16, NEXT)
                bank_ready(pe, at, ("x_turn", (g,)))
                for j in range(4):
                    r = pe.transpose(banks[6 + g % 2][:, j * P:(j + 1) * P],
                                     xin[:, 4 * h + j, k * P:(k + 1) * P], ident[:, :])
                r.then_inc(full_signal(at, ("x_turn", (g,))), 1)

            def project(at, name, which, h, m):
                if at.k0 == -1 and (name, h, m) == ("gate", 0, 0):
                    pe.wait_ge(sem("w_split"), 3)
                bank_read(pe, at, ("x_turn", (KC * h + 1,)), NEXT)
                bank_ready(pe, at, (name, (h, m)))
                dst = banks[6]
                pairs = [p for k in range(KC) for p in split(
                    lambda s: wr[:, s, which, k, m * P:(m + 1) * P], lambda s: (xh, xl)[s][:, h, k, :])]
                passes(dst, pairs).then_inc(full_signal(at, (name, (h, m))), 1)

            def x1_sum(at, g):
                h = g // 2
                batch_wait(pe, at, "hl_ready", 4, 2 * h + 2, NEXT)
                bank_ready(pe, at, ("x1_sum", (g,)))
                for t in range(2):
                    j = (2 * g + t) % 4
                    pairs = [(xs, w) for k in range(KC) for w, xs in split(
                        lambda s: wr[:, s, 2, k, :], lambda s: (xh, xl)[s][:, h, k, j * P:(j + 1) * P])]
                    r = passes(banks[6][:, t * C:(t + 1) * C], pairs)
                r.then_inc(full_signal(at, ("x1_sum", (g,))), 1)

            def x1_turn(at, g):
                h, k = divmod(g, KC)
                par = (at.k0 + NEXT) % 2
                batch_wait(pe, at, "x1_ready", NT, 4 * h + 4, NEXT)
                bank_ready(pe, at, ("x1_turn", (g,)))
                for j in range(4):
                    r = pe.transpose(banks[6][:, j * P:(j + 1) * P],
                                     x1[:, par, 4 * h + j, k * P:(k + 1) * P], ident[:, :])
                r.then_inc(full_signal(at, ("x1_turn", (g,))), 1)

            def logits(at):
                par = (at.k0 + NEXT) % 2
                if at.k0 == -1:
                    pe.wait_ge(sem("sim_normed"), 1)
                bank_ready(pe, at, ("logits", ()))
                for j in range(NT):
                    dst = banks[6][:, j * 2 * E:(j + 1) * 2 * E]
                    tok = slice(j * P, (j + 1) * P)
                    for n, (s, k) in enumerate(((0, 0), (0, 1), (1, 0), (1, 1))):
                        w = 2 * E if s == 0 else E
                        r = pe.matmul(dst[:, 0:w], lhsT=x1t[:, par, s * KC + k, tok], rhs=sn[:, k, 0:w],
                                      start=n == 0, stop=n == 3)
                r.then_inc(full_signal(at, ("logits", ())), 1)

            def mask_turn(at):
                batch_wait(pe, at, "mask_ready", 1, 1, NEXT)
                bank_ready(pe, at, ("mask_turn", ()))
                pe.transpose(banks[6].bitcast(bf16)[:, 0:P], maskb2[:, :, :, :].rearrange("p s t e -> p (s t e)"),
                             identb[:, :]).then_inc(full_signal(at, ("mask_turn", ())), 1)

            def mask(at, u):
                h, e = divmod(u, E)
                who = PLACE["mask", (u,)][1]
                par = (at.k0 + who) % 2
                bank_read(pe, at, ("mask_turn", ()), who)
                bank_ready(pe, at, ("mask", (u,)))
                pe.matmul(banks[3], lhsT=pick[:, e, :], rhs=spread[:, par, 4 * h:4 * h + 4, :].rearrange("p j t -> p (j t)"),
                          start=True, stop=True).then_inc(full_signal(at, ("mask", (u,))), 1)

            def qkv(at, u, o):
                h, e = divmod(u, E)
                slot = u % XM_RING
                if at.k0 == 0 and u == 0:
                    pe.wait_ge(sem("qkv_split"), o + 1)
                if o == 0:
                    batch_wait(pe, at, "xm_ready", UNITS, u + 1, THIS)
                if e == 0:
                    if o < 2:
                        batch_wait(pe, at, "qk_split", 4, 2 * h - 1 + o, THIS)
                    else:
                        batch_wait(pe, at, "vt_ready", 2, h, THIS)
                pairs = [p for k in range(KC) for p in split(
                    lambda s: wqkv[:, s, o, e, k, :], lambda s: xm[:, slot, s * KC + k, :])]
                r = passes(banks[o], pairs, first=e == 0, last=e == E - 1)
                if e == E - 1:
                    r.then_inc(sem("acc_full"), 1)
                elif o == 2:
                    r.then_inc(sem("xm_used"), 1)

            def v_turn(at, h):
                who = PLACE["v_turn", (h,)][1]
                batch_wait(pe, at, "vt_ready", 2, h + 1, who)
                bank_ready(pe, at, ("v_turn", (h,)))
                for j in range(4):
                    r = pe.transpose(banks[7][:, j * P:(j + 1) * P], vt[:, j * P:(j + 1) * P], ident[:, :])
                r.then_inc(full_signal(at, ("v_turn", (h,))), 1)

            def score(at, j):
                who = PLACE["score", (j,)][1]
                c, w = j // 4, (j + 1) * P
                batch_wait(pe, at, "qk_split", 4, 2 * c + 2, who)
                bank_ready(pe, at, ("score", (j,)))
                for lo in range(0, w, HT):
                    hi = min(w, lo + HT)
                    dst = wide[:, lo:hi] if c else banks[4 + j % 2][:, lo:hi]
                    pairs = split(lambda s: qk[:, s, 0, j * P:(j + 1) * P], lambda s: qk[:, s, 1, lo:hi])
                    diag = hi == w
                    passes(dst, pairs, last=not diag)
                    if diag:
                        r = pe.matmul(dst[:, hi - lo - P:hi - lo], lhsT=identb[:, :], rhs=causal[:, :], start=False, stop=True)
                r.then_inc(full_signal(at, ("score", (j,))), 1)

            def p_turn(at, j, part):
                who = PLACE["p_turn", (j, part)][1]
                bank_read(pe, at, ("score", (j,)), who)
                bank_ready(pe, at, ("p_turn", (j, part)))
                for n, kt in enumerate(range(4 * part, min(4 * part + 4, j + 1))):
                    r = pe.transpose(banks[7][:, n * P:(n + 1) * P], p32[:, j % 2, kt * P:(kt + 1) * P], ident[:, :])
                r.then_inc(full_signal(at, ("p_turn", (j, part))), 1)

            def pv(at, c):
                who = PLACE["pv", (c,)][1]
                bank_read(pe, at, ("p_turn", (4 * c + 3, c)), who)
                bank_ready(pe, at, ("pv", (c,)))
                tiles = 4 * c + 4
                for kt in range(tiles):
                    q0 = max(0, kt - 4 * c) * P
                    pairs = split(lambda s: v[:, s, kt, :], lambda s: pt[:, s, kt, q0:HT])
                    r = passes(banks[6][:, q0:HT], pairs, first=kt == 0, last=kt == tiles - 1)
                r.then_inc(full_signal(at, ("pv", (c,))), 1)

            def o_proj_part(at, j, part):
                who = PLACE["o_proj", (j, part)][1]
                if at.k0 == 0 and (j, part) == (0, 0):
                    pe.wait_ge(sem("o_split"), 1)
                bank_read(pe, at, ("pv", (j // 4,)), who)
                bank_ready(pe, at, ("o_proj", (j, part)))
                tok = slice((j % 4) * P, (j % 4 + 1) * P)
                pairs = [(at_, w) for w, at_ in split(
                    lambda s: wo_e[:, s, part * 2 * C:(part + 1) * 2 * C], lambda s: a[:, s, tok])]
                passes(banks[7 if part % 2 else 4 + part // 2], pairs).then_inc(full_signal(at, ("o_proj", (j, part))), 1)

            walk(pe, {
                "x_turn": x_turn, "gate": lambda at, h, m: project(at, "gate", 1, h, m),
                "inp": lambda at, h, m: project(at, "inp", 0, h, m), "x1_sum": x1_sum, "x1_turn": x1_turn,
                "logits": logits, "mask_turn": mask_turn, "mask": mask, "qkv": qkv, "v_turn": v_turn,
                "score": score, "p_turn": p_turn, "pv": pv, "o_proj": o_proj_part})

        @block.scalar
        def _(act):
            for n in range(3):
                act.wait_ge(sem("w_turned"), n + 1)
                act.activation(wr[:, 0, n, :, :].rearrange("p k c -> p (k c)"), banks[n], ACT.Copy).then_inc(sem("w_high"), 1)
            act.wait_ge(sem("small_loaded"), 80)
            act.activation(bias_g[:, 1, :], bias_g[:, 0, :], ACT.Copy, scale=0.5).then_inc(sem("bias_halved"), 1)
            act.activation(gate_sb[:, 1, :], gate_sb[:, 0, :], ACT.Tanh, scale=0.5).then_inc(sem("gates_tanh"), 1)
            act.wait_ge(sem("bias_halved"), 1)

            def w_high(at, n):
                if n == 3:
                    act.wait_ge(sem("o_loaded"), 16)
                    act.activation(wo_e[:, 0, :], o_raw, ACT.Copy).then_inc(sem("o_high"), 1)
                    return
                act.wait_ge(sem("qkv_loaded"), 48)
                act.activation(wqkv[:, 0, n, :, :, :].rearrange("p e k d -> p (e k d)"), (q_raw, k_raw, v_raw)[n],
                               ACT.Copy, scale=UP).then_inc(sem("qkv_high"), 1)

            def x_turn(at, g):
                h, k = divmod(g, KC)
                bank_read(act, at, ("x1_sum", (2 * h + 1,)), THIS)
                bank_full(act, at, ("x_turn", (g,)))
                act.activation(xh[:, h, k, :], banks[6 + g % 2], ACT.Copy).then_inc(sem("xh_ready"), 1)

            def gate(at, h, m):
                n = 2 * h + m
                batch_wait(act, at, "scanned", 4, n - 1, NEXT)
                bank_full(act, at, ("gate", (h, m)))
                act.activation(gbuf[:, m, :], banks[6], ACT.Tanh, bias=bias_g[:, 1, m:m + 1],
                               scale=0.5).then_inc(sem("free6"), 1)

            def h_split(at, h):
                for m in range(KC):
                    batch_wait(act, at, "scanned", 4, 2 * h + 2, NEXT)
                    act.activation(xh[:, h, m, :], hbuf[:, m, :], ACT.Copy).then_inc(sem("hh_ready"), 1)

            def ln_apply(at, h):
                par = (at.k0 + NEXT) % 2
                batch_wait(act, at, "ln_shift", 1, 1, NEXT)
                batch_wait(act, at, "tile_summed", NT, 2 * h + 2, PREV)
                for j in range(2 * h, 2 * h + 2):
                    act.activation(x1[:, par, j, :], xin[:, j, :], ACT.Identity, bias=shift[:, j:j + 1],
                                   scale=rs[:, j:j + 1]).then_inc(sem("x1_ready"), 1)

            def x1_turn(at, g):
                h, k = divmod(g, KC)
                par = (at.k0 + NEXT) % 2
                bank_full(act, at, ("x1_turn", (g,)))
                act.activation(x1t[:, par, k, h * HT:(h + 1) * HT], banks[6], ACT.Copy).then_inc(sem("x1h_ready"), 1)

            def route_soft(at):
                batch_wait(act, at, "route_shifted", 1, 1, NEXT)
                act.activation(rt[:, 6, :, :], rt[:, 5, :, :], ACT.Exp).then_inc(sem("route_exp"), 1)

            def mask(at, u):
                who = PLACE["mask", (u,)][1]
                batch_wait(act, at, "xm_ready", UNITS, u - MK_RING + 1, who)
                bank_full(act, at, ("mask", (u,)))
                act.activation(mk[:, u % MK_RING, :], banks[3], ACT.Copy).then_inc(sem("free3"), 1)

            def qkv_out(at, h, o):
                batch_wait(act, at, "acc_full", 6, 3 * h + o + 1, THIS)
                if o == 2:
                    act.activation(vt[:, :], banks[2], ACT.Copy, scale=DOWN).then_inc(sem("vt_ready"), 1)
                    return
                bank_read(act, at, ("score", (7,)), PREV)
                act.activation(qk[:, 0, o, h * HT:(h + 1) * HT], banks[o], ACT.Copy,
                               scale=QK_SCALE[o]).then_inc(sem("qk_high"), 1)

            def v_turn(at, h):
                bank_full(act, at, ("v_turn", (h,)))
                who = PLACE["v_turn", (h,)][1]
                bank_read(act, at, ("pv", (1,)), who - 1)
                act.activation(v[:, 0, 4 * h:4 * h + 4, :].rearrange("p n d -> p (n d)"), banks[7],
                               ACT.Copy).then_inc(sem("vh_ready"), 1)

            def exp(at, j):
                who = PLACE["score", (j,)][1]
                w = (j + 1) * P
                if j >= 2:
                    bank_full(act, at, ("p_turn", (j - 2, (j - 2) // 4)), who)
                batch_wait(act, at, "max_found", NT, j + 1, who)
                src = wide[:, 0:w] if j >= 4 else banks[4 + j % 2][:, 0:w]
                act.activation(p32[:, j % 2, 0:w], src, ACT.Exp, bias=negmax[:, j:j + 1],
                               accum_out=psums[:, j:j + 1]).then_inc(sem(bank_use("score", (j,))[2][0]), 1)

            def p_turn(at, j, part):
                who = PLACE["p_turn", (j, part)][1]
                n = min(4, j + 1 - 4 * part)
                c = j // 4
                bank_read(act, at, ("pv", (1 - c,)), who if c else who - 1)
                bank_full(act, at, ("p_turn", (j, part)))
                act.activation(pt[:, 0, 4 * part:4 * part + n, (j % 4) * P:(j % 4 + 1) * P],
                               banks[7][:, 0:n * P].rearrange("p (n q) -> p n q", n=n), ACT.Copy).then_inc(sem("pth_ready"), 1)

            def pv(at, c):
                who = PLACE["pv", (c,)][1]
                bank_read(act, at, ("o_proj", (3 if c else 7, 3)), who if c else who - 1)
                bank_full(act, at, ("pv", (c,)))
                act.activation(a[:, 0, :], banks[6], ACT.Copy).then_inc(sem("ah_ready"), 1)

            def o_proj_part(at, j, part):
                if part % 2 == 0:
                    return
                who = PLACE["o_proj", (j, part)][1]
                batch_wait(act, at, "weighed", 2, j // 4 + 1, who)
                bank_full(act, at, ("o_proj", (j, part)))
                for i in range(2):
                    n = 3 * j + part - 2 + i
                    if part == 1 and i == 0:
                        dst = side[:, j % 2, :]
                        batch_wait(act, at, "tile_summed", NT, j - 1, who)
                    else:
                        dst = tmp[:, n % TMP_RING, :]
                        batch_wait(act, at, "side_added", 3 * NT, n - TMP_RING + 1, who)
                    act.activation(dst, banks[7][:, i * C:(i + 1) * C], ACT.Copy,
                                   scale=cw[:, j, 2 * part + i:2 * part + i + 1]).then_inc(sem("side_scaled"), 1)

            def fin_norm(at, c):
                batch_wait(act, at, "fin_shift", 2, c + 1, PREV)
                for n in range(4):
                    j = 4 * c + n
                    act.activation(y[:, n, :], y[:, n, :], ACT.Identity, bias=shift2[:, j:j + 1],
                                   scale=rs2[:, j:j + 1]).then_inc(sem("y_ready"), 1)

            walk(act, {"x_turn": x_turn, "gate": gate, "h_split": h_split, "ln_apply": ln_apply, "x1_turn": x1_turn,
                       "route_soft": route_soft, "mask": mask, "qkv_out": qkv_out, "v_turn": v_turn,
                       "p_turn": p_turn, "pv": pv, "o_proj": o_proj_part, "fin_norm": fin_norm,
                       "w_high": w_high, "exp": exp})

        @block.vector
        def _(dve):
            dve.wait_ge(sem("small_loaded"), 80)
            dve.tensor_tensor(sim_sq[:, :, :], sim_sb[:, :, :], sim_sb[:, :, :], ALU.mult).then_inc(sem("sim_squared"), 1)
            for n in range(3):
                dve.wait_ge(sem("w_high"), n + 1)
                dve.tensor_tensor(wr[:, 1, n, :, :].rearrange("p k c -> p (k c)"), banks[n],
                                  wr[:, 0, n, :, :].rearrange("p k c -> p (k c)").bitcast(f32),
                                  ALU.subtract).then_inc(sem("w_split"), 1)
            dve.wait_ge(sem("sim_summed"), 1)
            dve.tensor_copy(sim_n[:, 0, :], banks[3][:, 0:E]).then_inc(sem("sim_sum_copied"), 1)
            dve.wait_ge(sem("sim_rooted"), 1)
            dve.tensor_scalar(sim_n[:, 2, :], sim_n[:, 1, :], NORM_FLOOR, DOWN, ALU.max, ALU.mult).then_inc(sem("prep"), 1)
            dve.wait_ge(sem("prep"), 1)
            dve.reciprocal(sim_n[:, 0, :], sim_n[:, 2, :]).then_inc(sem("prep"), 1)
            dve.wait_ge(sem("prep"), 2)
            dve.tensor_tensor(sim_sq[:, :, :], sim_sb[:, :, :], sim_n[:, 0, :].unsqueeze(1).to_broadcast([P, KC, E]),
                              ALU.mult).then_inc(sem("prep"), 1)
            dve.wait_ge(sem("prep"), 3)
            dve.tensor_copy(sn[:, :, 0:E], sim_sq[:, :, :]).then_inc(sem("prep"), 1)
            dve.wait_ge(sem("prep"), 4)
            dve.tensor_tensor(sn[:, :, E:2 * E], sim_sq[:, :, :], sn[:, :, 0:E], ALU.subtract).then_inc(sem("sim_normed"), 1)
            dve.wait_ge(sem("gates_tanh"), 1)
            dve.tensor_scalar(gate_sb[:, 2, :], gate_sb[:, 1, :], 0.5, 0.5, ALU.mult, ALU.add).then_inc(sem("prep"), 1)
            dve.wait_ge(sem("prep"), 5)
            dve.wait_ge(sem("masks_made"), 3)
            dve.reduce_sum(pick1[:, :], pick3[:, :, :], AX.X).then_inc(sem("prep"), 1)
            dve.wait_ge(sem("prep"), 6)
            dve.tensor_copy(pick[:, :, :], pick1[:, :].unsqueeze(2).to_broadcast([NT * E, E, P])).then_inc(sem("prep"), 1)

            def w_low(at, n):
                if n == 3:
                    dve.wait_ge(sem("o_high"), 1)
                    dve.tensor_tensor(wo_e[:, 1, :], o_raw, wo_e[:, 0, :].bitcast(f32),
                                      ALU.subtract).then_inc(sem("o_split"), 1)
                    return
                dve.wait_ge(sem("qkv_high"), n + 1)
                dve.scalar_tensor_tensor(wqkv[:, 1, n, :, :, :].rearrange("p e k d -> p (e k d)"), (q_raw, k_raw, v_raw)[n],
                                         UP, wqkv[:, 0, n, :, :, :].rearrange("p e k d -> p (e k d)"),
                                         ALU.mult, ALU.subtract).then_inc(sem("qkv_split"), 1)

            def x_turn(at, g):
                h, k = divmod(g, KC)
                batch_wait(dve, at, "xh_ready", 4, g + 1, NEXT)
                dve.tensor_tensor(xl[:, h, k, :], banks[6 + g % 2], xh[:, h, k, :].bitcast(f32),
                                  ALU.subtract).then_inc(sem(f"free{6 + g % 2}"), 1)

            def inp(at, h, m):
                n = 2 * h + m
                bank_read(dve, at, ("gate", (h, m)), NEXT)
                batch_wait(dve, at, "scanned", 4, n, NEXT)
                dve.tensor_scalar(vbuf[:, :], gbuf[:, m, :], -0.5, 0.5, ALU.mult, ALU.add).then_inc(sem("gates_out"), 1)
                batch_wait(dve, at, "gates_out", 8, 2 * n + 1, NEXT)
                dve.tensor_scalar(gbuf[:, m, :], gbuf[:, m, :], 0.5, 0.5, ALU.mult, ALU.add).then_inc(sem("gates_out"), 1)
                bank_full(dve, at, ("inp", (h, m)))
                dve.scalar_tensor_tensor(vbuf[:, :], banks[6], bias_i[:, m:m + 1], vbuf[:, :],
                                         ALU.add, ALU.mult).then_inc(sem("free6"), 1)
                batch_wait(dve, at, "gates_out", 8, 2 * n + 2, NEXT)
                bank_read(dve, at, ("inp", (h, m)), NEXT)
                if h:
                    batch_wait(dve, at, "hh_ready", 4, 2, NEXT)
                    batch_wait(dve, at, "scanned", 4, m + 1, NEXT)
                else:
                    batch_wait(dve, at, "hh_ready", 4, 0, NEXT)
                dve.tensor_tensor_scan(hbuf[:, m, :], gbuf[:, m, :], vbuf[:, :],
                                       hbuf[:, m, HT - 1:HT] if h else 0.0, ALU.mult, ALU.add).then_inc(sem("scanned"), 1)

            def h_split(at, h):
                for m in range(KC):
                    batch_wait(dve, at, "hh_ready", 4, 2 * h + m + 1, NEXT)
                    dve.tensor_tensor(xl[:, h, m, :], hbuf[:, m, :], xh[:, h, m, :].bitcast(f32),
                                      ALU.subtract).then_inc(sem("hl_ready"), 1)

            def x1_sum(at, g):
                bank_full(dve, at, ("x1_sum", (g,)))
                batch_wait(dve, at, "xb_ready", 1, 1, NEXT)
                two = xin[:, 2 * g:2 * g + 2, :].rearrange("p j c -> p (j c)")
                dve.tensor_tensor(two, banks[6], two, ALU.add).then_inc(sem("free6"), 1)
                bank_read(dve, at, ("x1_sum", (g,)), NEXT)
                for j in (2 * g, 2 * g + 1):
                    dve.bn_stats(st[:, j, :], xin[:, j, :]).then_inc(sem("ln_partial"), 1)

            def ln(at):
                alone(dve)
                batch_wait(dve, at, "ln_partial", NT, NT, NEXT)
                for j in range(NT):
                    r = dve.bn_aggr(mv[:, j, :], st[:, j, :])
                r.then_inc(sem("ln_stats"), 1)

            def ln_apply(at, h):
                if h:
                    return
                batch_wait(dve, at, "ln_rstd", 1, 1, NEXT)
                dve.scalar_tensor_tensor(shift[:, :], mv[:, :, 0], -1.0, rs[:, 0:NT], ALU.mult, ALU.mult).then_inc(sem("ln_shift"), 1)
                dve.tensor_tensor(rnorm[:, 0, :], rs[:, NT:2 * NT], rs[:, 0:NT], ALU.mult).then_inc(sem("norm_step"), 1)
                batch_wait(dve, at, "norm_step", 3, 1, NEXT)
                dve.tensor_scalar(rnorm[:, 1, :], rnorm[:, 0, :], NORM_FLOOR, UP, ALU.max, ALU.mult).then_inc(sem("norm_step"), 1)
                batch_wait(dve, at, "norm_step", 3, 2, NEXT)
                dve.reciprocal(rnorm[:, 2, :], rnorm[:, 1, :]).then_inc(sem("norm_step"), 1)

            def x1_turn(at, g):
                h, k = divmod(g, KC)
                par = (at.k0 + NEXT) % 2
                tok = slice(h * HT, (h + 1) * HT)
                batch_wait(dve, at, "x1h_ready", 4, g + 1, NEXT)
                dve.tensor_tensor(x1t[:, par, KC + k, tok], banks[6], x1t[:, par, k, tok],
                                  ALU.subtract).then_inc(sem("free6"), 1)

            def logits(at):
                bank_full(dve, at, ("logits", ()))
                dve.reduce_sum(rt[:, 7, :, :], banks[6][:, 0:NT * 2 * E].rearrange("p (t s e) -> p t e s", t=NT, s=2),
                               AX.X).then_inc(sem("free6"), 1)

            STEPS = 15
            per_tile = [P, NT, E]
            logit, gated, active, fb, rank, masked, ex = (rt[:, n, :, :] for n in (0, 1, 2, 3, 4, 5, 6))

            def stepper(at, first):
                n = [first]

                def step(r):
                    r.then_inc(sem("route_step"), 1)
                    n[0] += 1
                    k = n[0]
                    batch_wait(dve, at, "route_step", STEPS, k, NEXT)
                return step

            def route_mask(at):
                step = stepper(at, 0)
                batch_wait(dve, at, "norm_step", 3, 3, NEXT)
                bank_read(dve, at, ("logits", ()), NEXT)
                step(dve.tensor_tensor(rt[:, 8, :, :], rt[:, 7, :, :], rnorm[:, 2, :].unsqueeze(2).to_broadcast(per_tile), ALU.mult))
                step(dve.tensor_tensor(logit, rt[:, 8, :, :], gate_sb[:, 2, :].unsqueeze(1).to_broadcast(per_tile), ALU.subtract))
                step(dve.tensor_scalar(active, logit, 0.0, None, ALU.is_gt))
                step(dve.reduce_max(rv[:, 0, :], active, AX.X))
                quad = [P, NT, E, E]
                above = cmp2[:, 0, :, :].rearrange("p t (e j) -> p t e j", e=E)
                equal = cmp2[:, 1, :, :].rearrange("p t (e j) -> p t e j", e=E)
                theirs, mine = logit.unsqueeze(2).to_broadcast(quad), logit.unsqueeze(3).to_broadcast(quad)
                step(dve.tensor_tensor(above, theirs, mine, ALU.is_gt))
                step(dve.tensor_tensor(equal, theirs, mine, ALU.is_equal))
                step(dve.tensor_tensor(equal, equal, earlier[:, :, :].unsqueeze(1).to_broadcast(quad), ALU.mult))
                step(dve.tensor_tensor(above, above, equal, ALU.add))
                step(dve.reduce_sum(rank, above, AX.X))
                step(dve.tensor_scalar(rv[:, 1, :], rv[:, 0, :], -1.0, 1.0, ALU.mult, ALU.add))
                step(dve.scalar_tensor_tensor(fb, rank, 2.0, rv[:, 1, :].unsqueeze(2).to_broadcast(per_tile), ALU.is_lt, ALU.mult))
                dve.tensor_tensor(maskb, active, fb, ALU.max).then_inc(sem("mask_ready"), 1)

            def mask_turn(at):
                par = (at.k0 + NEXT) % 2
                bank_full(dve, at, ("mask_turn", ()))
                src = banks[6].bitcast(bf16)[0:NT * E, 0:P].unsqueeze(1).to_broadcast([NT * E, NT, P])
                dve.tensor_tensor(spread[:, par, :, :], src, own_tile[:, :].unsqueeze(2).to_broadcast([NT * E, NT, P]),
                                  ALU.mult).then_inc(sem("free6"), 1)

            def route_max(at):
                step = stepper(at, 11)
                batch_wait(dve, at, "mask_ready", 1, 1, NEXT)
                step(dve.tensor_scalar(gated, logit, 0.0, None, ALU.max))
                step(dve.tensor_scalar(rt[:, 9, :, :], maskb, OFF, -OFF, ALU.mult, ALU.add))
                step(dve.tensor_tensor(rt[:, 7, :, :], rt[:, 9, :, :], gated, ALU.add))
                step(dve.reduce_max(rv[:, 2, :], rt[:, 7, :, :], AX.X))
                dve.tensor_tensor(masked, rt[:, 7, :, :], rv[:, 2, :].unsqueeze(2).to_broadcast(per_tile),
                                  ALU.subtract).then_inc(sem("route_shifted"), 1)

            def route_soft(at):
                par = (at.k0 + NEXT) % 2
                batch_wait(dve, at, "route_exp", 1, 1, NEXT)
                dve.reduce_sum(rv[:, 3, :], ex, AX.X).then_inc(sem("soft_step"), 1)
                batch_wait(dve, at, "soft_step", 3, 1, NEXT)
                dve.reciprocal(rv[:, 4, :], rv[:, 3, :]).then_inc(sem("soft_step"), 1)
                batch_wait(dve, at, "soft_step", 3, 2, NEXT)
                dve.tensor_tensor(rt[:, 8, :, :], ex, rv[:, 4, :].unsqueeze(2).to_broadcast(per_tile),
                                  ALU.mult).then_inc(sem("soft_step"), 1)
                batch_wait(dve, at, "soft_step", 3, 3, NEXT)
                dve.tensor_tensor(gw[:, par, :, :], rt[:, 8, :, :], maskb, ALU.mult).then_inc(sem("gw_ready"), 1)

            def mask(at, u):
                h, e = divmod(u, E)
                who = PLACE["mask", (u,)][1]
                par = (at.k0 + who) % 2
                bank_read(dve, at, ("mask", (u,)), who)
                old = u - XM_RING
                if old % E == E - 1:
                    batch_wait(dve, at, "acc_full", 6, 3 * (old // E) + 3, who)
                else:
                    done = lambda k: k // E * (E - 1) + k % E + 1
                    batch_wait(dve, at, "xm_used", 2 * (E - 1), done(old), who)
                dve.tensor_tensor(xm[:, u % XM_RING, :, :], x1t[:, par, :, h * HT:(h + 1) * HT],
                                  mk[:, u % MK_RING, :].unsqueeze(1).to_broadcast([P, 2 * KC, HT]),
                                  ALU.mult).then_inc(sem("xm_ready"), 1)

            def qkv_out(at, h, o):
                if o == 2:
                    return
                tok = slice(h * HT, (h + 1) * HT)
                batch_wait(dve, at, "qk_high", 4, 2 * h + o + 1, THIS)
                dve.scalar_tensor_tensor(qk[:, 1, o, tok], banks[o], QK_SCALE[o], qk[:, 0, o, tok].bitcast(f32),
                                         ALU.mult, ALU.subtract).then_inc(sem("qk_split"), 1)

            def v_turn(at, h):
                who = PLACE["v_turn", (h,)][1]
                batch_wait(dve, at, "vh_ready", 2, h + 1, who)
                dve.tensor_tensor(v[:, 1, 4 * h:4 * h + 4, :].rearrange("p n d -> p (n d)"), banks[7],
                                  v[:, 0, 4 * h:4 * h + 4, :].rearrange("p n d -> p (n d)"), ALU.subtract).then_inc(sem("free7"), 1)

            def score(at, j):
                who = PLACE["score", (j,)][1]
                w = (j + 1) * P
                bank_full(dve, at, ("score", (j,)))
                src = wide[:, 0:w] if j >= 4 else banks[4 + j % 2][:, 0:w]
                dve.reduce_max(negmax[:, j:j + 1], src, AX.X, negate=True).then_inc(sem("max_found"), 1)

            def p_turn(at, j, part):
                who = PLACE["p_turn", (j, part)][1]
                n = min(4, j + 1 - 4 * part)
                k = j + 1 if j < 4 else 4 + 2 * (j - 4) + part + 1
                batch_wait(dve, at, "pth_ready", 12, k, who)
                dst = (slice(None), slice(4 * part, 4 * part + n), slice((j % 4) * P, (j % 4 + 1) * P))
                dve.tensor_tensor(pt[:, 1, dst[1], dst[2]], banks[7][:, 0:n * P].rearrange("p (n q) -> p n q", n=n),
                                  pt[:, 0, dst[1], dst[2]], ALU.subtract).then_inc(sem("free7"), 1)

            def pv(at, c):
                who = PLACE["pv", (c,)][1]
                batch_wait(dve, at, "ah_ready", 2, c + 1, who)
                dve.tensor_tensor(a[:, 1, :], banks[6], a[:, 0, :].bitcast(f32), ALU.subtract).then_inc(sem("free6"), 1)

            def weigh(at, c):
                who = PLACE["weigh", (c,)][1]
                par = (at.k0 + who) % 2
                t4 = slice(4 * c, 4 * c + 4)
                bank_read(dve, at, ("score", (4 * c + 3,)), who)
                batch_wait(dve, at, "gw_ready", 1, 1, who)
                dve.reciprocal(pinv[:, t4], psums[:, t4]).then_inc(sem("sum_inverted"), 1)
                batch_wait(dve, at, "sum_inverted", 2, c + 1, who)
                dve.tensor_tensor(cw[:, t4, :], gw[:, par, t4, :], pinv[:, t4].unsqueeze(2).to_broadcast([P, 4, E]),
                                  ALU.mult).then_inc(sem("weighed"), 1)

            def o_proj_part(at, j, part):
                if part % 2:
                    return
                who = PLACE["o_proj", (j, part)][1]
                par = (at.k0 + who) % 2
                batch_wait(dve, at, "weighed", 2, j // 4 + 1, who)
                bank_full(dve, at, ("o_proj", (j, part)))
                for i in range(2):
                    batch_wait(dve, at, "main_added", 4 * NT, 4 * j + part + i, who)
                    dve.scalar_tensor_tensor(x1[:, par, j, :], banks[4 + part // 2][:, i * C:(i + 1) * C],
                                             cw[:, j, 2 * part + i:2 * part + i + 1], x1[:, par, j, :],
                                             ALU.mult, ALU.add).then_inc(sem("main_added"), 1)

            def tile_end(at, j):
                who = PLACE["tile_end", (j,)][1]
                par = (at.k0 + who) % 2
                batch_wait(dve, at, "main_added", 4 * NT, 4 * j + 4, who)
                batch_wait(dve, at, "side_added", 3 * NT, 3 * j + 3, who)
                if j % 4 == 0:
                    batch_wait(dve, at, "y_free", 2 * 16, 16 * (j // 4 + 1), who)
                dve.tensor_tensor(y[:, j % 4, :], x1[:, par, j, :], side[:, j % 2, :], ALU.add).then_inc(sem("tile_summed"), 1)
                batch_wait(dve, at, "tile_summed", NT, j + 1, who)
                dve.bn_stats(st2[:, j, :], y[:, j % 4, :]).then_inc(sem("fin_partial"), 1)
                alone(dve)
                batch_wait(dve, at, "fin_partial", NT, j + 1, who)
                dve.bn_aggr(mv2[:, j, :], st2[:, j, :]).then_inc(sem("fin_stats"), 1)

            def fin_norm(at, c):
                t4 = slice(4 * c, 4 * c + 4)
                batch_wait(dve, at, "fin_rstd", 2, c + 1, PREV)
                dve.scalar_tensor_tensor(shift2[:, t4], mv2[:, t4, 0], -1.0, rs2[:, t4], ALU.mult,
                                         ALU.mult).then_inc(sem("fin_shift"), 1)

            walk(dve, {"x_turn": x_turn, "inp": inp, "h_split": h_split, "x1_sum": x1_sum, "ln": ln, "ln_apply": ln_apply,
                       "x1_turn": x1_turn, "logits": logits, "route_mask": route_mask, "mask_turn": mask_turn, "route_max": route_max,
                       "route_soft": route_soft, "mask": mask, "qkv_out": qkv_out, "v_turn": v_turn, "score": score,
                       "p_turn": p_turn, "pv": pv, "weigh": weigh, "o_proj": o_proj_part, "tile_end": tile_end,
                       "fin_norm": fin_norm, "w_low": w_low})

        @block.gpsimd
        def _(pool):
            pool.memset(ident[:, :], 0.0).then_inc(sem("cleared"), 1)
            pool.memset(causal[:, :], 0.0).then_inc(sem("cleared"), 1)
            pool.memset(earlier[:, :, :], 1.0).then_inc(sem("cleared"), 1)
            pool.memset(pick3[:, :, :], 0.0).then_inc(sem("cleared"), 1)
            pool.memset(own_tile[:, :], 1.0).then_inc(sem("cleared"), 1)
            pool.memset(halves[:, 0:NT], -0.5).then_inc(sem("cleared"), 1)
            pool.memset(halves[:, NT:2 * NT], 0.5).then_inc(sem("cleared"), 1)
            pool.memset(ones, 1.0).then_inc(sem("cleared"), 1)
            pool.memset(epsilons[:, :], EPS).then_inc(sem("cleared"), 1)
            pool.memset(channels[:, :], float(C)).then_inc(sem("cleared"), 1)
            pool.memset(maskb2[:, 1, :, :], 0.0).then_inc(sem("cleared"), 1)
            pool.wait_ge(sem("cleared"), 11)
            pool.affine_select(out=ident[:, :], in_=ident[:, :], compare_op=ALU.not_equal, fill=1.0, base=0,
                               pattern=[[-1, P]], channel_multiplier=1).then_inc(sem("selected"), 1)
            pool.wait_ge(sem("selected"), 1)
            pool.tensor_copy(identb[:, :], ident[:, :]).then_inc(sem("consts"), 1)
            pool.affine_select(out=causal[:, :], in_=causal[:, :], compare_op=ALU.is_ge, fill=CAUSAL, base=0,
                               pattern=[[-1, P]], channel_multiplier=1).then_inc(sem("selected"), 1)
            pool.affine_select(out=earlier[:, :, :], in_=earlier[:, :, :], compare_op=ALU.is_gt, fill=0.0, base=0,
                               pattern=[[1, E], [-1, E]], channel_multiplier=0).then_inc(sem("masks_made"), 1)
            pool.affine_select(out=pick3[:, :, :], in_=pick3[:, :, :], compare_op=ALU.not_equal, fill=1.0, base=0,
                               pattern=[[-1, E], [-E, NT]], channel_multiplier=1).then_inc(sem("masks_made"), 1)
            pool.affine_select(out=own_tile[:, :], in_=own_tile[:, :], compare_op=ALU.is_ge, fill=0.0, base=0,
                               pattern=[[-E, NT]], channel_multiplier=1).then_inc(sem("selected"), 1)
            pool.wait_ge(sem("selected"), 3)
            pool.affine_select(out=own_tile[:, :], in_=own_tile[:, :], compare_op=ALU.is_ge, fill=0.0, base=E - 1,
                               pattern=[[E, NT]], channel_multiplier=-1).then_inc(sem("masks_made"), 1)
            pool.wait_ge(sem("sim_sum_copied"), 1)
            pool.tensor_tensor(sim_n[:, 1, :], sim_n[:, 0, :], halves[:, NT:NT + E], ALU.pow).then_inc(sem("sim_rooted"), 1)
            pool.wait_ge(sem("small_loaded"), 80)

            def x_turn(at, g):
                if g < 3:
                    return
                for k in (2, 3):
                    bank_full(pool, at, ("x_turn", (k,)))
                pool.tensor_tensor(xin[:, :, :], xin[:, :, :], bias_o[:, :].unsqueeze(1).to_broadcast([P, NT, C]),
                                   ALU.add).then_inc(sem("xb_ready"), 1)

            def ln(at):
                batch_wait(pool, at, "ln_stats", 1, 1, NEXT)
                pool.tensor_tensor(vp[:, 0:NT], mv[:, :, 1], epsilons[:, :], ALU.add).then_inc(sem("ln_var"), 1)
                pool.tensor_tensor(vp[:, NT:2 * NT], mv[:, :, 1], channels[:, :], ALU.mult).then_inc(sem("ln_var"), 1)
                batch_wait(pool, at, "ln_var", 2, 2, NEXT)
                pool.tensor_tensor(rs[:, :], vp[:, :], halves[:, :], ALU.pow).then_inc(sem("ln_rstd"), 1)

            def o_proj_part(at, j, part):
                if part % 2 == 0:
                    return
                who = PLACE["o_proj", (j, part)][1]
                for i in range(part == 1, 2):
                    n = 3 * j + part - 2 + i
                    batch_wait(pool, at, "side_scaled", 4 * NT, 4 * j + part + i, who)
                    if n % 3:
                        batch_wait(pool, at, "side_added", 3 * NT, n, who)
                    pool.tensor_tensor(side[:, j % 2, :], side[:, j % 2, :], tmp[:, n % TMP_RING, :],
                                       ALU.add).then_inc(sem("side_added"), 1)

            def fin(at, c):
                t4 = slice(4 * c, 4 * c + 4)
                batch_wait(pool, at, "fin_stats", NT, 4 * c + 4, PREV)
                pool.tensor_tensor(vp2[:, t4], mv2[:, t4, 1], epsilons[:, t4], ALU.add).then_inc(sem("fin_var"), 1)
                batch_wait(pool, at, "fin_var", 2, c + 1, PREV)
                pool.tensor_tensor(rs2[:, t4], vp2[:, t4], halves[:, 0:4], ALU.pow).then_inc(sem("fin_rstd"), 1)

            walk(pool, {"x_turn": x_turn, "ln": ln, "o_proj": o_proj_part, "fin": fin})


_INS = ["L0_attn_x", "L0_attn_Wi", "L0_attn_bi", "L0_attn_Wg", "L0_attn_bg", "L0_attn_Wo", "L0_attn_bo",
        "L0_ffn_sim_matrix", "L0_ffn_gates", "L0_ffn_q_proj", "L0_ffn_k_proj", "L0_ffn_v_proj", "L0_ffn_o_proj"]
_OUTS = [((B, T, C), "float32")]


def kernel(**inputs):
    import concourse.bacc as _bacc
    from concourse.bass_utils import run_bass_kernel_spmd as _run

    nc = _bacc.Bacc("TRN2", target_bir_lowering=False, num_devices=1)
    arrays, args = {}, []
    for name in _INS:
        arr = np.ascontiguousarray(inputs[name])
        arrays[f"in_{name}_dram"] = arr
        args.append(nc.dram_tensor(f"in_{name}_dram", arr.shape, mybir.dt.from_np(arr.dtype), kind="ExternalInput").ap())
    for i, (shape, dtype) in enumerate(_OUTS):
        args.append(nc.dram_tensor(f"out_{i}_dram", shape, mybir.dt.from_np(np.dtype(dtype)), kind="ExternalOutput").ap())
    rglru_moe(nc, *args)
    r = _run(nc, [arrays], core_ids=[0])
    return r.results[0]["out_0_dram"]
```

```python
import concourse.bass as bass
import numpy as np
from concourse import mybir
from contextlib import ExitStack

B, T, C = 16, 1024, 256
E, D = 8, 128
P = 128
NT = T // P
HT = T // 2
KC = C // P
UNITS = 2 * E
EPS = 1e-5
NORM_FLOOR = 1e-12
UP = 2.0 ** 8
DOWN = 2.0 ** -8
QK_SCALE = (DOWN * float(D) ** -0.5, DOWN)
OFF = 1e9
CAUSAL = -3.0e38
PREV, THIS, NEXT = -1, 0, 1
FIRST = "first"

XM_RING, MK_RING, TMP_RING = 4, 4, 3


def order():
    gaps = {
        0: [("x_load", (), NEXT), ("v_turn", (1,), PREV), ("score", (4,), PREV)],
        1: [("x_turn", (0,), NEXT), ("fin", (0,), PREV)],
        2: [("exp", (4,), PREV), ("x_turn", (1,), NEXT)],
        3: [("score", (5,), PREV), ("x_turn", (2,), NEXT)],
        4: [("x_turn", (3,), NEXT), ("exp", (5,), PREV), ("biases", (), FIRST)],
        5: [("p_turn", (4, 0), PREV), ("gate", (0, 0), NEXT)],
        6: [("p_turn", (4, 1), PREV), ("score", (6,), PREV), ("inp", (0, 0), NEXT)],
        7: [("gate", (0, 1), NEXT), ("exp", (6,), PREV)],
        8: [("p_turn", (5, 0), PREV), ("inp", (0, 1), NEXT), ("sim_sum", (), FIRST)],
        9: [("p_turn", (5, 1), PREV), ("score", (7,), PREV), ("h_split", (0,), NEXT), ("gate", (1, 0), NEXT)],
        10: [("inp", (1, 0), NEXT), ("exp", (7,), PREV)],
        11: [("p_turn", (6, 0), PREV), ("gate", (1, 1), NEXT)],
        12: [("p_turn", (6, 1), PREV)],
        13: [("p_turn", (7, 0), PREV), ("inp", (1, 1), NEXT)],
        14: [("p_turn", (7, 1), PREV), ("x1_sum", (0,), NEXT), ("h_split", (1,), NEXT)],
        15: [("x1_sum", (1,), NEXT), ("fin_norm", (0,), PREV)],
        16: [("pv", (1,), PREV), ("weigh", (1,), PREV)],
        17: [("w_high", (n,), FIRST) for n in range(2)],
        20: [("ln", (0,), NEXT), ("x1_sum", (2,), NEXT), ("ln_shift", (0,), NEXT)],
        21: [("x1_sum", (3,), NEXT)],
        23: [("ln", (1,), NEXT), ("sim_norm", (), FIRST)],
        25: [("score", (0,), THIS), ("ln_apply", (0,), NEXT), ("ln_shift", (1,), NEXT)],
        26: [("v_turn", (0,), THIS), ("score", (1,), THIS), ("exp", (0,), THIS), ("ln_apply", (1,), NEXT)],
        27: [("exp", (1,), THIS), ("ln_apply", (2,), NEXT)],
        28: [("norm_root", (), NEXT), ("p_turn", (0, 0), THIS), ("score", (2,), THIS), ("x1_turn", (0,), NEXT)],
        29: [("p_turn", (1, 0), THIS), ("score", (3,), THIS), ("exp", (2,), THIS), ("x1_turn", (1,), NEXT), ("w_low", (0,), FIRST)],
        30: [("exp", (3,), THIS), ("ln_apply", (3,), NEXT), ("fin", (1,), PREV)],
        31: [("x1_turn", (2,), NEXT), ("p_turn", (2, 0), THIS)],
        32: [("x1_turn", (3,), NEXT), ("p_turn", (3, 0), THIS)],
        33: [("logits", (), NEXT), ("fin_norm", (1,), PREV), ("w_high", (2,), FIRST), ("w_high", (3,), FIRST)],
        34: [("pv", (0,), THIS), ("weigh", (0,), THIS), ("route_mask", (), NEXT)],
        39: [("mask_turn", (), NEXT), ("mask_load", (0,), NEXT), ("mask_load", (1,), NEXT), ("route_max", (), NEXT)],
        41: [("route_soft", (), NEXT), ("w_low", (1,), FIRST)],
        43: [("w_low", (2,), FIRST)],
        46: [("w_low", (3,), FIRST)],
    }
    for start, end, tiles, who in ((18, 25.9, range(4, 8), PREV), (37.8, 48, range(4), THIS)):
        first = {}
        for n, (tile, part) in enumerate((t, p) for t in tiles for p in range(4)):
            at = start + (end - start) * n / 16
            before = first.setdefault(int(at), 0)
            gaps.setdefault(int(at), []).insert(before, ("o_proj", (tile, part), who))
            first[int(at)] += 1
            if part == 3:
                gap, late = (int(at) + 2) % 48, int(at) + 2 >= 48
                gaps.setdefault(gap, []).insert(0, ("tile_end", (tile,), who - late))
                first[gap] = first.get(gap, 0) + 1
    steps = []
    for u in range(UNITS):
        half, slot = divmod(u, E)
        ahead = u + 2
        steps.append(("mask", (ahead % UNITS,), THIS if ahead < UNITS else NEXT))
        ahead = u + 5
        if ahead % 2 == 0 and ahead - UNITS not in (0, 2):
            steps.append(("mask_load", (ahead % UNITS // 2,), THIS if ahead < UNITS else NEXT))
        for o in range(3):
            steps.append(("qkv", (u, o), THIS))
            if slot == E - 1:
                steps.append(("qkv_out", (half, o), THIS))
            steps += gaps.get(3 * u + o, [])
    return steps


def last_order(steps):
    mine = [s for s in steps if s[2] == PREV]
    late = [("tile_end", (j,), PREV) for j in range(4)] + [("fin", (0,), PREV)]
    late = [s for s in mine if s in late]
    attention = [("score", (4,)), ("v_turn", (1,)), ("score", (5,)), ("score", (6,)), ("exp", (4,)), ("exp", (5,)),
                 ("p_turn", (4, 0)), ("p_turn", (4, 1)), ("score", (7,)), ("exp", (6,)),
                 ("p_turn", (5, 0)), ("p_turn", (5, 1)), ("pv_tile", (4,)), ("exp", (7,)),
                 ("p_turn", (6, 0)), ("p_turn", (6, 1)), ("pv_tile", (5,)),
                 ("p_turn", (7, 0)), ("p_turn", (7, 1)), ("pv_tile", (6,))]
    attention = [(name, args, PREV) for name, args in attention]
    return late + attention + [s for s in mine if s not in late + attention]


ORDER = order()
LAST_ORDER = last_order(ORDER)
ITERATIONS = range(-1, B + 1)


def steps_of(it):
    return LAST_ORDER if it == B else ORDER


def bank_use(name, args, it):
    last = it == B
    spare = it == B - 1
    signal, reads = None, 1
    if name == "score":
        bank = 4 + args[0] % 2 if args[0] < 4 else {5: 0, 6: 2}.get(args[0], 4) if last else 4
    elif name == "o_proj":
        if args[1] % 2:
            bank, signal, reads = 3 if last and args[1] == 3 else 7, "side_scaled", 2
        else:
            bank, signal, reads = (0 if last and args[0] % 2 else 4) + args[1] // 2, "main_added", 2
    elif name == "x_turn":
        bank = (6, 3, 7, 3)[args[0]]
    elif name in ("x1_sum", "x1_turn"):
        bank = 3 if args[0] % 2 else 6
    elif name == "p_turn":
        bank = (6 if last else 3 if spare else 7) if args[1] else 7
    elif name == "v_turn":
        bank = 7 if args[0] else 3
    elif name == "pv":
        bank = 0 if last else 6
    elif name == "mask_turn":
        bank, signal = 3, "mask_turned"
    elif name in ("gate", "inp", "logits"):
        bank = 3 if name == "inp" else 6
    else:
        return None
    wide = name == "score" and args[0] >= 4
    return (bank, bank + 1) if wide else (bank,), f"full{bank}", (signal or f"free{bank}",) * reads


def count_banks():
    count, last, ahead, full, freed = {}, {}, {}, {}, {}
    for it in ITERATIONS:
        for name, args, who in steps_of(it):
            job = name, args
            use = bank_use(name, args, it)
            if use is None or who == FIRST or not 0 <= it + who < B:
                continue
            banks, signal, frees = use
            need = {}
            for k in banks:
                for s, v in last.get(k, {}).items():
                    need[s] = max(need.get(s, 0), v)
            ahead[it, job] = need
            count[signal] = count.get(signal, 0) + 1
            full[it, job] = (signal, count[signal])
            for s in frees:
                count[s] = count.get(s, 0) + 1
            freed[it, job] = {s: count[s] for s in frees}
            for k in banks:
                last[k] = freed[it, job]
    return ahead, full, freed


AHEAD, FULL, FREED = count_banks()
BATCH = {(name, args): who for name, args, who in ORDER}
LOOP_FIRST, LOOP_PAIRS = 1, 7


class At:

    def __init__(self, k0, turn=None):
        self.k0, self.turn = k0, turn

    def count(self, of):
        here = of(self.k0)
        if self.turn is None:
            return here
        step = of(self.k0 + 2) - here
        return self.turn * step + here if step else here

    def has(self, who):
        return self.k0 == -1 if who == FIRST else 0 <= self.k0 + who < B

    def wait(self, eng, sem, of):
        if of(self.k0) > 0:
            eng.wait_ge(sem, self.count(of))


def rglru_moe(nc, x, Wi, bi, Wg, bg, Wo, bo, sim, gates, q_proj, k_proj, v_proj, o_proj, out):
    f32, f32r, f16, bf16 = mybir.dt.float32, mybir.dt.float32r, mybir.dt.float16, mybir.dt.bfloat16
    ALU, ACT, AX = mybir.AluOpType, mybir.ActivationFunctionType, mybir.AxisListType

    ctx = ExitStack()
    with ctx:
        def sb(name, shape, dt):
            return ctx.enter_context(nc.sbuf_tensor(name, shape, dt))

        sems = {}

        def sem(name):
            if name not in sems:
                sems[name] = ctx.enter_context(nc.semaphore(name))
            return sems[name]

        ident = sb("ident", [P, P], f32)
        identb = sb("identb", [P, P], bf16)
        causal = sb("causal", [P, P], bf16)
        earlier = sb("earlier", [P, E, E], f32)
        halves = sb("halves", [P, 2 * NT], f32)
        wr = sb("wr", [P, 2, 3, KC, C], f32r)
        wqkv = sb("wqkv", [P, 2, 3, E, KC, D], f16)
        wo_e = sb("wo_e", [P, 2, E * C], f32r)
        sn = sb("sn", [P, KC, 2 * E], f16)
        sim_sb = sb("sim_sb", [P, KC, E], f32)
        sim_sq = sb("sim_sq", [P, KC, E], f32)
        sim_n = sb("sim_n", [P, 3, E], f32)
        gate_sb = sb("gate_sb", [P, 3, E], f32)
        bias_i = sb("bias_i", [P, KC], f32)
        bias_g = sb("bias_g", [P, 2, KC], f32)
        bias_o = sb("bias_o", [P, C], f32)
        xin = sb("xin", [P, NT, C], f32)
        xh = sb("xh", [P, 2, KC, HT], f32r)
        xl = sb("xl", [P, 2, KC, HT], f32r)
        gbuf = sb("gbuf", [P, 2, HT], f32)
        vbuf = sb("vbuf", [P, HT], f32)
        hbuf = sb("hbuf", [P, KC, HT], f32)
        x1 = sb("x1", [P, 2, NT, C], f32)
        x1t = sb("x1t", [P, 2, 2 * KC, T], f16)
        st = sb("st", [P, NT, 6], f32)
        mv = sb("mv", [P, NT, 2], f32)
        vp = sb("vp", [P, 2 * NT], f32)
        rs = sb("rs", [P, 2 * NT], f32)
        shift = sb("shift", [P, NT], f32)
        rnorm = sb("rnorm", [P, 3, NT], f32)
        rt = sb("rt", [P, 6, NT, E], f32)
        cmp2 = gbuf[:, :, :].rearrange("p s (t q) -> p s t q", t=NT)
        rv = sb("rv", [P, 5, NT], f32)
        maskb2 = sb("maskb2", [P, 2, E, NT], bf16)
        maskb = maskb2[:, 0, :, :].rearrange("p e t -> p t e")
        epsilons = sb("epsilons", [P, NT], f32)
        channels = sb("channels", [P, NT], f32)
        gw = sb("gw", [P, 2, NT, E], f32)
        maskt = sb("maskt", [E * NT, P], f16)
        mask_rows = nc.dram_tensor("mask_rows", [2, E, T], f16).ap()
        mk = sb("mk", [P, MK_RING, 2, HT], f16)
        xm32 = sb("xm32", [P, XM_RING * 2 * KC * HT // 2], f32)
        xm = xm32[:, :].bitcast(f16).rearrange("p (r s t) -> p r s t", r=XM_RING, s=2 * KC)
        qk = sb("qk", [P, 2, 2, T], f32r)
        vt = sb("vt", [P, HT], f32)
        v = sb("v", [P, 2, NT, D], f16)
        p32 = sb("p32", [P, 2, T], f32)
        pt32 = sb("pt32", [P, 2 * NT * HT // 2], f32)
        pt = pt32[:, :].bitcast(f16).rearrange("p (s n t) -> p s n t", s=2, n=NT)
        negmax = sb("negmax", [P, NT], f32)
        psums = sb("psums", [P, NT], f32)
        pinv = sb("pinv", [P, NT], f32)
        cw = sb("cw", [P, NT, E], f32)
        a = sb("a", [P, 2, HT], f32r)
        tmp = sb("tmp", [P, TMP_RING, C], f32)
        ones = tmp[:, 0, 0:P]
        side = sb("side", [P, 2, C], f32)
        st2 = sb("st2", [P, NT, 6], f32)
        mv2 = sb("mv2", [P, NT, 2], f32)
        vp2 = sb("vp2", [P, NT], f32)
        rs2 = sb("rs2", [P, NT], f32)
        shift2 = sb("shift2", [P, NT], f32)
        y = sb("y", [P, 4, C], f32)

        w_raw = p32[:, :, :].rearrange("p a t -> p (a t)")[:, 0:3 * KC * C].rearrange(
            "p (w m c) -> p w m c", w=3, m=KC)
        q_raw, k_raw = (xm32[:, n * 2048:(n + 1) * 2048] for n in range(2))
        v_raw, o_raw = (pt32[:, n * 2048:(n + 1) * 2048] for n in range(2))

        psum = [ctx.enter_context(nc.psum_tensor(f"banks{n}{n + 1}", [P, T], f32)) for n in (0, 2, 4, 6)]
        banks = [psum[n // 2][:, n % 2 * HT:(n % 2 + 1) * HT] for n in range(8)]

        x_v = x.rearrange("b (j p) c -> b p j c", p=P)
        out_v = out.rearrange("b (j p) c -> b p j c", p=P)

        def bank_ready(eng, at, job):
            for s in AHEAD[at.k0, job]:
                at.wait(eng, sem(s), lambda it: AHEAD[it, job][s])

        def bank_full(eng, at, job, who=None):
            back = 0 if who is None else who - BATCH[job]
            at.wait(eng, sem(FULL[at.k0 + back, job][0]), lambda it: FULL[it + back, job][1])

        def bank_read(eng, at, job, who):
            back = who - BATCH[job]
            if (at.k0 + back, job) not in FREED:
                return
            for s in FREED[at.k0 + back, job]:
                at.wait(eng, sem(s), lambda it: FREED[it + back, job][s])

        def bank_of(at, job):
            use = bank_use(*job, at.k0)[0]
            return psum[use[0] // 2] if len(use) == 2 else banks[use[0]]

        def free_signal(at, job):
            return sem(bank_use(*job, at.k0)[2][0])

        def full_signal(at, job):
            return sem(FULL[at.k0, job][0])

        def batch_wait(eng, at, name, per_batch, k, who):
            at.wait(eng, sem(name), lambda it: per_batch * (it + who) + k)

        def alone(eng):
            eng.wait_ge(sem("consts"), 1)

        def walk(eng, parts):
            def iteration(at):
                for name, args, who in steps_of(at.k0):
                    if name in parts and at.has(who):
                        parts[name](at, *args)
            for it in range(-1, LOOP_FIRST):
                iteration(At(it))
            with eng.Fori(0, LOOP_PAIRS) as turn:
                iteration(At(LOOP_FIRST, turn))
                iteration(At(LOOP_FIRST + 1, turn))
            for it in range(LOOP_FIRST + 2 * LOOP_PAIRS, B + 1):
                iteration(At(it))

        block = ctx.enter_context(nc.Block())

        @block.sync
        def _(sp):
            sp.sem_inc(sem("y_free"), 16)
            for n, w in enumerate((Wi, Wg, Wo)):
                sp.dma_start(w_raw[:, n, :, :], w.rearrange("(m p) c -> p m c", p=P)).then_inc(sem("w_loaded"), 16)
            sp.dma_start(xin[:, 0:4, :], x_v[0][:, 0:4, :]).then_inc(sem("x_half_loaded"), 16)
            sp.dma_start(xin[:, 4:8, :], x_v[0][:, 4:8, :]).then_inc(sem("x_loaded"), 16)
            with nc.allow_non_contiguous_dma(reason="a few hundred values"):
                sp.dma_start(bias_i[:, :], bi.rearrange("(m p) -> p m", p=P)).then_inc(sem("small_loaded"), 16)
                sp.dma_start(bias_g[:, 0, :], bg.rearrange("(m p) -> p m", p=P)).then_inc(sem("small_loaded"), 16)
            sp.dma_start(bias_o[:, :], bo.partition_broadcast(P)).then_inc(sem("small_loaded"), 16)
            sp.dma_start(gate_sb[:, 0, :], gates.partition_broadcast(P)).then_inc(sem("small_loaded"), 16)
            sp.dma_start(sim_sb[:, :, :], sim.rearrange("(k p) e -> p k e", p=P)).then_inc(sem("small_loaded"), 16)
            for raw, w in ((q_raw, q_proj), (k_raw, k_proj), (v_raw, v_proj)):
                sp.dma_start(raw.rearrange("p (e k d) -> p e k d", e=E, k=KC),
                             w.rearrange("e (k p) d -> p e k d", p=P)).then_inc(sem("qkv_loaded"), 16)
            sp.dma_start(o_raw.rearrange("p (e c) -> p e c", e=E),
                         o_proj.rearrange("e d c -> d e c")).then_inc(sem("o_loaded"), 16)

            def x_load(at):
                if at.k0 == -1:
                    return
                batch_wait(sp, at, "x1_ready", NT, 0, NEXT)
                b = at.count(lambda it: it + NEXT)
                src = x_v[b] if at.turn is None else x_v[bass.ds(b, 1)][0]
                sp.dma_start(xin[:, :, :], src).then_inc(sem("x_loaded"), 16)

            def fin_norm(at, c):
                b = at.count(lambda it: it + PREV)
                if at.k0 == B and c == 1:
                    for n in (0, 2):
                        batch_wait(sp, at, "y_ready", 8, 4 * c + n + 2, PREV)
                        sp.dma_start(out_v[b][:, 4 * c + n:4 * c + n + 2, :], y[:, n:n + 2, :]).then_inc(sem("y_free"), 16)
                    return
                batch_wait(sp, at, "y_ready", 8, 4 * c + 4, PREV)
                dst = out_v[b] if at.turn is None else out_v[bass.ds(b, 1)][0]
                sp.dma_start(dst[:, 4 * c:4 * c + 4, :], y[:, :, :]).then_inc(sem("y_free"), 16)

            def mask_turn(at):
                par = (at.k0 + NEXT) % 2
                batch_wait(sp, at, "mask_turned", 1, 1, NEXT)
                sp.dma_start(mask_rows[par].rearrange("e (t p) -> (e t) p", p=P), maskt[:, :]).then_inc(sem("mask_stored"), 16)

            def mask_load(at, n):
                who = BATCH["mask_load", (n,)]
                par = (at.k0 + who) % 2
                h, e = divmod(2 * n, E)
                if n == 0:
                    batch_wait(sp, at, "mask_stored", 16, 16, who)
                else:
                    batch_wait(sp, at, "xm_ready", UNITS, 2 * (n - MK_RING) + 2, who)
                src = mask_rows[par, e:e + 2, h * HT:(h + 1) * HT]
                sp.dma_start(mk[:, n % MK_RING, :, :], src.partition_broadcast(P)).then_inc(sem(f"mask_loaded{n % MK_RING}"), 16)

            walk(sp, {"x_load": x_load, "fin_norm": fin_norm, "mask_turn": mask_turn, "mask_load": mask_load})
            sp.wait_ge(sem("y_free"), 16 * (2 * B + 2))

        @block.tensor
        def _(pe):
            def passes(dst, pairs, first=True, last=True):
                for n, (w, m) in enumerate(pairs):
                    r = pe.matmul(dst, lhsT=w, rhs=m, start=first and n == 0, stop=last and n == len(pairs) - 1)
                return r

            def split(w, m):
                return [(w(0), m(0)), (w(1), m(0)), (w(0), m(1))]

            pe.wait_ge(sem("consts"), 1)
            pe.wait_ge(sem("w_loaded"), 48)
            for n in range(3):
                for k in range(KC):
                    for m in range(KC):
                        r = pe.transpose(banks[n][:, k * C + m * P:k * C + (m + 1) * P],
                                         w_raw[:, n, m, k * P:(k + 1) * P], ident[:, :])
                r.then_inc(sem("w_turned"), 1)

            def sim_sum(at):
                pe.wait_ge(sem("sim_squared"), 1)
                for k in range(KC):
                    r = pe.matmul(banks[4][:, 0:E], lhsT=ones, rhs=sim_sq[:, k, :], start=k == 0, stop=k == KC - 1)
                r.then_inc(sem("sim_summed"), 1)

            def x_turn(at, g):
                h, k = divmod(g, KC)
                if at.k0 == -1 and h == 0:
                    pe.wait_ge(sem("x_half_loaded"), 16)
                else:
                    batch_wait(pe, at, "x_loaded", 16, 16, NEXT)
                bank_ready(pe, at, ("x_turn", (g,)))
                for j in range(4):
                    r = pe.transpose(bank_of(at, ("x_turn", (g,)))[:, j * P:(j + 1) * P],
                                     xin[:, 4 * h + j, k * P:(k + 1) * P], ident[:, :])
                r.then_inc(full_signal(at, ("x_turn", (g,))), 1)

            def project(at, name, which, h, m):
                if at.k0 == -1 and (name, h, m) == ("gate", 0, 0):
                    pe.wait_ge(sem("w_split"), 3)
                if (name, m) == ("gate", 0):
                    if h:
                        bank_read(pe, at, ("x_turn", (2,)), NEXT)
                    bank_read(pe, at, ("x_turn", (2 * h + 1,)), NEXT)
                bank_ready(pe, at, (name, (h, m)))
                dst = bank_of(at, (name, (h, m)))
                pairs = [p for k in range(KC) for p in split(
                    lambda s: wr[:, s, which, k, m * P:(m + 1) * P], lambda s: (xh, xl)[s][:, h, k, :])]
                passes(dst, pairs).then_inc(full_signal(at, (name, (h, m))), 1)

            def x1_sum(at, g):
                h = g // 2
                batch_wait(pe, at, "hl_ready", 4, 2 * h + 2, NEXT)
                bank_ready(pe, at, ("x1_sum", (g,)))
                for t in range(2):
                    j = (2 * g + t) % 4
                    pairs = [(xs, w) for k in range(KC) for w, xs in split(
                        lambda s: wr[:, s, 2, k, :], lambda s: (xh, xl)[s][:, h, k, j * P:(j + 1) * P])]
                    r = passes(bank_of(at, ("x1_sum", (g,)))[:, t * C:(t + 1) * C], pairs)
                r.then_inc(full_signal(at, ("x1_sum", (g,))), 1)

            def x1_turn(at, g):
                h, k = divmod(g, KC)
                par = (at.k0 + NEXT) % 2
                batch_wait(pe, at, "x1_ready", NT, 4 * h + 4, NEXT)
                bank_ready(pe, at, ("x1_turn", (g,)))
                for j in range(4):
                    r = pe.transpose(bank_of(at, ("x1_turn", (g,)))[:, j * P:(j + 1) * P],
                                     x1[:, par, 4 * h + j, k * P:(k + 1) * P], ident[:, :])
                r.then_inc(full_signal(at, ("x1_turn", (g,))), 1)

            def logits(at):
                par = (at.k0 + NEXT) % 2
                if at.k0 == -1:
                    pe.wait_ge(sem("sim_normed"), 1)
                bank_read(pe, at, ("x1_turn", (3,)), NEXT)
                bank_ready(pe, at, ("logits", ()))
                for j in range(NT):
                    dst = banks[6][:, j * 2 * E:(j + 1) * 2 * E]
                    tok = slice(j * P, (j + 1) * P)
                    for n, (s, k) in enumerate(((0, 0), (0, 1), (1, 0), (1, 1))):
                        w = 2 * E if s == 0 else E
                        r = pe.matmul(dst[:, 0:w], lhsT=x1t[:, par, s * KC + k, tok], rhs=sn[:, k, 0:w],
                                      start=n == 0, stop=n == 3)
                r.then_inc(full_signal(at, ("logits", ())), 1)

            def mask_turn(at):
                batch_wait(pe, at, "mask_ready", 1, 1, NEXT)
                bank_ready(pe, at, ("mask_turn", ()))
                pe.transpose(banks[3].bitcast(bf16)[:, 0:P], maskb2[:, :, :, :].rearrange("p s e t -> p (s e t)"),
                             identb[:, :]).then_inc(full_signal(at, ("mask_turn", ())), 1)

            def qkv(at, u, o):
                h, e = divmod(u, E)
                slot = u % XM_RING
                if at.k0 == 0 and u == 0:
                    pe.wait_ge(sem("qkv_split"), o + 1)
                if o == 0:
                    batch_wait(pe, at, "xm_ready", UNITS, u + 1, THIS)
                if e == 0:
                    if o < 2:
                        batch_wait(pe, at, "qk_split", 4, 2 * h - 1 + o, THIS)
                    else:
                        batch_wait(pe, at, "vt_ready", 2, h, THIS)
                pairs = [p for k in range(KC) for p in split(
                    lambda s: wqkv[:, s, o, e, k, :], lambda s: xm[:, slot, s * KC + k, :])]
                r = passes(banks[o], pairs, first=e == 0, last=e == E - 1)
                if e == E - 1:
                    r.then_inc(sem("acc_full"), 1)
                elif o == 2:
                    r.then_inc(sem("xm_used"), 1)

            def v_turn(at, h):
                who = BATCH["v_turn", (h,)]
                batch_wait(pe, at, "vt_ready", 2, h + 1, who)
                bank_ready(pe, at, ("v_turn", (h,)))
                for j in range(4):
                    r = pe.transpose(bank_of(at, ("v_turn", (h,)))[:, j * P:(j + 1) * P], vt[:, j * P:(j + 1) * P], ident[:, :])
                r.then_inc(full_signal(at, ("v_turn", (h,))), 1)

            def score(at, j):
                who = BATCH["score", (j,)]
                c, w = j // 4, (j + 1) * P
                batch_wait(pe, at, "qk_split", 4, 2 * c + 2, who)
                bank_ready(pe, at, ("score", (j,)))
                for lo in range(0, w, HT):
                    hi = min(w, lo + HT)
                    dst = bank_of(at, ("score", (j,)))[:, lo:hi]
                    pairs = split(lambda s: qk[:, s, 0, j * P:(j + 1) * P], lambda s: qk[:, s, 1, lo:hi])
                    diag = hi == w
                    passes(dst, pairs, last=not diag)
                    if diag:
                        r = pe.matmul(dst[:, hi - lo - P:hi - lo], lhsT=identb[:, :], rhs=causal[:, :], start=False, stop=True)
                r.then_inc(full_signal(at, ("score", (j,))), 1)

            def p_turn(at, j, part):
                who = BATCH["p_turn", (j, part)]
                bank_read(pe, at, ("score", (j,)), who)
                bank_ready(pe, at, ("p_turn", (j, part)))
                for n, kt in enumerate(range(4 * part, min(4 * part + 4, j + 1))):
                    r = pe.transpose(bank_of(at, ("p_turn", (j, part)))[:, n * P:(n + 1) * P], p32[:, j % 2, kt * P:(kt + 1) * P], ident[:, :])
                r.then_inc(full_signal(at, ("p_turn", (j, part))), 1)

            def pv_tile(at, j):
                for part in range(j // 4 + 1):
                    bank_read(pe, at, ("p_turn", (j, part)), PREV)
                if j == 4:
                    bank_ready(pe, at, ("pv", (1,)))
                q = slice((j % 4) * P, (j % 4 + 1) * P)
                for kt in range(j + 1):
                    pairs = split(lambda s: v[:, s, kt, :], lambda s: pt[:, s, kt, q])
                    r = passes(bank_of(at, ("pv", (1,)))[:, q], pairs, first=kt == 0, last=kt == j)
                return r

            def pv(at, c):
                who = BATCH["pv", (c,)]
                if at.k0 == B:
                    pv_tile(at, 4 * c + 3).then_inc(full_signal(at, ("pv", (c,))), 1)
                    return
                if at.k0 == B - 1 and c:
                    bank_read(pe, at, ("p_turn", (4 * c + 3, 0)), who)
                bank_read(pe, at, ("p_turn", (4 * c + 3, c)), who)
                bank_ready(pe, at, ("pv", (c,)))
                tiles = 4 * c + 4
                for kt in range(tiles):
                    q0 = max(0, kt - 4 * c) * P
                    pairs = split(lambda s: v[:, s, kt, :], lambda s: pt[:, s, kt, q0:HT])
                    r = passes(bank_of(at, ("pv", (c,)))[:, q0:HT], pairs, first=kt == 0, last=kt == tiles - 1)
                r.then_inc(full_signal(at, ("pv", (c,))), 1)

            def o_proj_part(at, j, part):
                who = BATCH["o_proj", (j, part)]
                if at.k0 == 0 and (j, part) == (0, 0):
                    pe.wait_ge(sem("o_split"), 1)
                bank_read(pe, at, ("pv", (j // 4,)), who)
                bank_ready(pe, at, ("o_proj", (j, part)))
                tok = slice((j % 4) * P, (j % 4 + 1) * P)
                pairs = [(at_, w) for w, at_ in split(
                    lambda s: wo_e[:, s, part * 2 * C:(part + 1) * 2 * C], lambda s: a[:, s, tok])]
                passes(bank_of(at, ("o_proj", (j, part))), pairs).then_inc(full_signal(at, ("o_proj", (j, part))), 1)

            walk(pe, {
                "sim_sum": sim_sum,
                "x_turn": x_turn, "gate": lambda at, h, m: project(at, "gate", 1, h, m),
                "inp": lambda at, h, m: project(at, "inp", 0, h, m), "x1_sum": x1_sum, "x1_turn": x1_turn,
                "logits": logits, "mask_turn": mask_turn, "qkv": qkv, "v_turn": v_turn,
                "score": score, "p_turn": p_turn, "pv_tile": pv_tile, "pv": pv, "o_proj": o_proj_part})

        @block.scalar
        def _(act):
            for n in range(3):
                act.wait_ge(sem("w_turned"), n + 1)
                act.activation(wr[:, 0, n, :, :].rearrange("p k c -> p (k c)"), banks[n], ACT.Copy).then_inc(sem("w_high"), 1)

            def biases(at):
                act.wait_ge(sem("small_loaded"), 80)
                act.activation(bias_g[:, 1, :], bias_g[:, 0, :], ACT.Copy, scale=0.5).then_inc(sem("bias_halved"), 1)
                act.activation(gate_sb[:, 1, :], gate_sb[:, 0, :], ACT.Tanh, scale=0.5).then_inc(sem("gates_tanh"), 1)
                act.wait_ge(sem("bias_halved"), 1)

            def w_high(at, n):
                if n == 3:
                    act.wait_ge(sem("o_loaded"), 16)
                    act.activation(wo_e[:, 0, :], o_raw, ACT.Copy).then_inc(sem("o_high"), 1)
                    return
                act.wait_ge(sem("qkv_loaded"), 48)
                act.activation(wqkv[:, 0, n, :, :, :].rearrange("p e k d -> p (e k d)"), (q_raw, k_raw, v_raw)[n],
                               ACT.Copy, scale=UP).then_inc(sem("qkv_high"), 1)

            def x_turn(at, g):
                h, k = divmod(g, KC)
                bank_read(act, at, ("x1_sum", (2 * h + 1,)), THIS)
                bank_full(act, at, ("x_turn", (g,)))
                act.activation(xh[:, h, k, :], bank_of(at, ("x_turn", (g,))), ACT.Copy).then_inc(sem("xh_ready"), 1)

            def gate(at, h, m):
                n = 2 * h + m
                batch_wait(act, at, "scanned", 4, n - 1, NEXT)
                bank_full(act, at, ("gate", (h, m)))
                act.activation(gbuf[:, m, :], banks[6], ACT.Tanh, bias=bias_g[:, 1, m:m + 1],
                               scale=0.5).then_inc(sem("free6"), 1)

            def h_split(at, h):
                for m in range(KC):
                    batch_wait(act, at, "scanned", 4, 2 * h + 2, NEXT)
                    act.activation(xh[:, h, m, :], hbuf[:, m, :], ACT.Copy).then_inc(sem("hh_ready"), 1)

            def ln_apply(at, h):
                par = (at.k0 + NEXT) % 2
                batch_wait(act, at, "ln_shift", 2, h // 2 + 1, NEXT)
                batch_wait(act, at, "tile_summed", NT, 2 * h + 2, PREV)
                for j in range(2 * h, 2 * h + 2):
                    act.activation(x1[:, par, j, :], xin[:, j, :], ACT.Identity, bias=shift[:, j:j + 1],
                                   scale=rs[:, j:j + 1]).then_inc(sem("x1_ready"), 1)

            def x1_turn(at, g):
                h, k = divmod(g, KC)
                par = (at.k0 + NEXT) % 2
                bank_full(act, at, ("x1_turn", (g,)))
                act.activation(x1t[:, par, k, h * HT:(h + 1) * HT], bank_of(at, ("x1_turn", (g,))), ACT.Copy).then_inc(sem("x1h_ready"), 1)

            def route_soft(at):
                batch_wait(act, at, "route_shifted", 1, 1, NEXT)
                act.activation(rt[:, 5, :, :], rt[:, 5, :, :], ACT.Exp).then_inc(sem("route_exp"), 1)

            def qkv_out(at, h, o):
                batch_wait(act, at, "acc_full", 6, 3 * h + o + 1, THIS)
                if o == 2:
                    act.activation(vt[:, :], banks[2], ACT.Copy, scale=DOWN).then_inc(sem("vt_ready"), 1)
                    return
                bank_read(act, at, ("score", (7,)), PREV)
                act.activation(qk[:, 0, o, h * HT:(h + 1) * HT], banks[o], ACT.Copy,
                               scale=QK_SCALE[o]).then_inc(sem("qk_high"), 1)

            def v_turn(at, h):
                bank_full(act, at, ("v_turn", (h,)))
                who = BATCH["v_turn", (h,)]
                bank_read(act, at, ("pv", (1,)), who - 1)
                act.activation(v[:, 0, 4 * h:4 * h + 4, :].rearrange("p n d -> p (n d)"), bank_of(at, ("v_turn", (h,))),
                               ACT.Copy).then_inc(sem("vh_ready"), 1)

            def exp(at, j):
                who = BATCH["score", (j,)]
                w = (j + 1) * P
                if j >= 2:
                    bank_full(act, at, ("p_turn", (j - 2, (j - 2) // 4)), who)
                batch_wait(act, at, "max_found", NT, j + 1, who)
                src = bank_of(at, ("score", (j,)))[:, 0:w]
                act.activation(p32[:, j % 2, 0:w], src, ACT.Exp, bias=negmax[:, j:j + 1],
                               accum_out=psums[:, j:j + 1]).then_inc(free_signal(at, ("score", (j,))), 1)

            def p_turn(at, j, part):
                who = BATCH["p_turn", (j, part)]
                n = min(4, j + 1 - 4 * part)
                c = j // 4
                bank_read(act, at, ("pv", (1 - c,)), who if c else who - 1)
                bank_full(act, at, ("p_turn", (j, part)))
                act.activation(pt[:, 0, 4 * part:4 * part + n, (j % 4) * P:(j % 4 + 1) * P],
                               bank_of(at, ("p_turn", (j, part)))[:, 0:n * P].rearrange("p (n q) -> p n q", n=n), ACT.Copy).then_inc(sem("pth_ready"), 1)

            def pv(at, c):
                who = BATCH["pv", (c,)]
                bank_read(act, at, ("o_proj", (3 if c else 7, 3)), who if c else who - 1)
                bank_full(act, at, ("pv", (c,)))
                act.activation(a[:, 0, :], bank_of(at, ("pv", (c,))), ACT.Copy).then_inc(sem("ah_ready"), 1)

            def o_proj_part(at, j, part):
                if part % 2 == 0:
                    return
                who = BATCH["o_proj", (j, part)]
                batch_wait(act, at, "weighed", 2, j // 4 + 1, who)
                bank_full(act, at, ("o_proj", (j, part)))
                for i in range(2):
                    n = 3 * j + part - 2 + i
                    if part == 1 and i == 0:
                        dst = side[:, j % 2, :]
                        batch_wait(act, at, "tile_summed", NT, j - 1, who)
                    else:
                        dst = tmp[:, n % TMP_RING, :]
                        batch_wait(act, at, "side_added", 3 * NT, n - TMP_RING + 1, who)
                    act.activation(dst, bank_of(at, ("o_proj", (j, part)))[:, i * C:(i + 1) * C], ACT.Copy,
                                   scale=cw[:, j, 2 * part + i:2 * part + i + 1]).then_inc(sem("side_scaled"), 1)

            def fin_norm(at, c):
                batch_wait(act, at, "fin_shift", 2, c + 1, PREV)
                for n in range(4):
                    j = 4 * c + n
                    act.activation(y[:, n, :], y[:, n, :], ACT.Identity, bias=shift2[:, j:j + 1],
                                   scale=rs2[:, j:j + 1]).then_inc(sem("y_ready"), 1)

            walk(act, {"biases": biases, "x_turn": x_turn, "gate": gate, "h_split": h_split, "ln_apply": ln_apply, "x1_turn": x1_turn,
                       "route_soft": route_soft, "qkv_out": qkv_out, "v_turn": v_turn,
                       "p_turn": p_turn, "pv": pv, "o_proj": o_proj_part, "fin_norm": fin_norm,
                       "w_high": w_high, "exp": exp})

        @block.vector
        def _(dve):
            for n in range(3):
                dve.wait_ge(sem("w_high"), n + 1)
                dve.tensor_tensor(wr[:, 1, n, :, :].rearrange("p k c -> p (k c)"), banks[n],
                                  wr[:, 0, n, :, :].rearrange("p k c -> p (k c)").bitcast(f32),
                                  ALU.subtract).then_inc(sem("w_split"), 1)

            def biases(at):
                dve.wait_ge(sem("small_loaded"), 80)
                dve.tensor_tensor(sim_sq[:, :, :], sim_sb[:, :, :], sim_sb[:, :, :], ALU.mult).then_inc(sem("sim_squared"), 1)

            def sim_sum(at):
                dve.wait_ge(sem("sim_summed"), 1)
                dve.tensor_copy(sim_n[:, 0, :], banks[4][:, 0:E]).then_inc(sem("sim_sum_copied"), 1)

            def sim_norm(at):
                dve.wait_ge(sem("sim_rooted"), 1)
                dve.tensor_scalar(sim_n[:, 2, :], sim_n[:, 1, :], NORM_FLOOR, DOWN, ALU.max, ALU.mult).then_inc(sem("prep"), 1)
                dve.wait_ge(sem("prep"), 1)
                dve.reciprocal(sim_n[:, 0, :], sim_n[:, 2, :]).then_inc(sem("prep"), 1)
                dve.wait_ge(sem("prep"), 2)
                dve.tensor_tensor(sim_sq[:, :, :], sim_sb[:, :, :], sim_n[:, 0, :].unsqueeze(1).to_broadcast([P, KC, E]),
                                  ALU.mult).then_inc(sem("prep"), 1)
                dve.wait_ge(sem("prep"), 3)
                dve.tensor_copy(sn[:, :, 0:E], sim_sq[:, :, :]).then_inc(sem("prep"), 1)
                dve.wait_ge(sem("prep"), 4)
                dve.tensor_tensor(sn[:, :, E:2 * E], sim_sq[:, :, :], sn[:, :, 0:E], ALU.subtract).then_inc(sem("sim_normed"), 1)
                dve.wait_ge(sem("gates_tanh"), 1)
                dve.tensor_scalar(gate_sb[:, 2, :], gate_sb[:, 1, :], 0.5, 0.5, ALU.mult, ALU.add).then_inc(sem("prep"), 1)
                dve.wait_ge(sem("prep"), 5)
                dve.wait_ge(sem("masks_made"), 2)

            def w_low(at, n):
                if n == 3:
                    dve.wait_ge(sem("o_high"), 1)
                    dve.tensor_tensor(wo_e[:, 1, :], o_raw, wo_e[:, 0, :].bitcast(f32),
                                      ALU.subtract).then_inc(sem("o_split"), 1)
                    return
                dve.wait_ge(sem("qkv_high"), n + 1)
                dve.scalar_tensor_tensor(wqkv[:, 1, n, :, :, :].rearrange("p e k d -> p (e k d)"), (q_raw, k_raw, v_raw)[n],
                                         UP, wqkv[:, 0, n, :, :, :].rearrange("p e k d -> p (e k d)"),
                                         ALU.mult, ALU.subtract).then_inc(sem("qkv_split"), 1)

            def x_turn(at, g):
                h, k = divmod(g, KC)
                batch_wait(dve, at, "xh_ready", 4, g + 1, NEXT)
                dve.tensor_tensor(xl[:, h, k, :], bank_of(at, ("x_turn", (g,))), xh[:, h, k, :].bitcast(f32),
                                  ALU.subtract).then_inc(free_signal(at, ("x_turn", (g,))), 1)

            def inp(at, h, m):
                n = 2 * h + m
                bank_read(dve, at, ("gate", (h, m)), NEXT)
                batch_wait(dve, at, "scanned", 4, n, NEXT)
                dve.tensor_scalar(vbuf[:, :], gbuf[:, m, :], -0.5, 0.5, ALU.mult, ALU.add).then_inc(sem("gates_out"), 1)
                batch_wait(dve, at, "gates_out", 8, 2 * n + 1, NEXT)
                dve.tensor_scalar(gbuf[:, m, :], gbuf[:, m, :], 0.5, 0.5, ALU.mult, ALU.add).then_inc(sem("gates_out"), 1)
                bank_full(dve, at, ("inp", (h, m)))
                dve.scalar_tensor_tensor(vbuf[:, :], banks[3], bias_i[:, m:m + 1], vbuf[:, :],
                                         ALU.add, ALU.mult).then_inc(sem("free3"), 1)
                batch_wait(dve, at, "gates_out", 8, 2 * n + 2, NEXT)
                bank_read(dve, at, ("inp", (h, m)), NEXT)
                if h:
                    batch_wait(dve, at, "hh_ready", 4, 2, NEXT)
                    batch_wait(dve, at, "scanned", 4, m + 1, NEXT)
                else:
                    batch_wait(dve, at, "hh_ready", 4, 0, NEXT)
                dve.tensor_tensor_scan(hbuf[:, m, :], gbuf[:, m, :], vbuf[:, :],
                                       hbuf[:, m, HT - 1:HT] if h else 0.0, ALU.mult, ALU.add).then_inc(sem("scanned"), 1)

            def h_split(at, h):
                for m in range(KC):
                    batch_wait(dve, at, "hh_ready", 4, 2 * h + m + 1, NEXT)
                    dve.tensor_tensor(xl[:, h, m, :], hbuf[:, m, :], xh[:, h, m, :].bitcast(f32),
                                      ALU.subtract).then_inc(sem("hl_ready"), 1)

            def x1_sum(at, g):
                bank_full(dve, at, ("x1_sum", (g,)))
                batch_wait(dve, at, "xb_ready", 1, 1, NEXT)
                two = xin[:, 2 * g:2 * g + 2, :].rearrange("p j c -> p (j c)")
                job = ("x1_sum", (g,))
                dve.tensor_tensor(two, bank_of(at, job), two, ALU.add).then_inc(free_signal(at, job), 1)
                bank_read(dve, at, ("x1_sum", (g,)), NEXT)
                for j in (2 * g, 2 * g + 1):
                    dve.bn_stats(st[:, j, :], xin[:, j, :]).then_inc(sem("ln_partial"), 1)

            def ln(at, c):
                alone(dve)
                batch_wait(dve, at, "ln_partial", NT, 4 * c + 4, NEXT)
                for j in range(4 * c, 4 * c + 4):
                    r = dve.bn_aggr(mv[:, j, :], st[:, j, :])
                r.then_inc(sem("ln_stats"), 1)

            def ln_shift(at, c):
                t4 = slice(4 * c, 4 * c + 4)
                batch_wait(dve, at, "ln_rstd", 2, c + 1, NEXT)
                dve.scalar_tensor_tensor(shift[:, t4], mv[:, t4, 0], -1.0, rs[:, t4], ALU.mult, ALU.mult).then_inc(sem("ln_shift"), 1)

            def norm_root(at):
                batch_wait(dve, at, "norm_rooted", 1, 1, NEXT)
                dve.tensor_tensor(rnorm[:, 0, :], rs[:, NT:2 * NT], rs[:, 0:NT], ALU.mult).then_inc(sem("norm_step"), 1)
                batch_wait(dve, at, "norm_step", 3, 1, NEXT)
                dve.tensor_scalar(rnorm[:, 1, :], rnorm[:, 0, :], NORM_FLOOR, UP, ALU.max, ALU.mult).then_inc(sem("norm_step"), 1)
                batch_wait(dve, at, "norm_step", 3, 2, NEXT)
                dve.reciprocal(rnorm[:, 2, :], rnorm[:, 1, :]).then_inc(sem("norm_step"), 1)

            def x1_turn(at, g):
                h, k = divmod(g, KC)
                par = (at.k0 + NEXT) % 2
                tok = slice(h * HT, (h + 1) * HT)
                batch_wait(dve, at, "x1h_ready", 4, g + 1, NEXT)
                job = ("x1_turn", (g,))
                dve.tensor_tensor(x1t[:, par, KC + k, tok], bank_of(at, job), x1t[:, par, k, tok],
                                  ALU.subtract).then_inc(free_signal(at, job), 1)

            def logits(at):
                bank_full(dve, at, ("logits", ()))
                dve.reduce_sum(rt[:, 4, :, :], banks[6][:, 0:NT * 2 * E].rearrange("p (t s e) -> p t e s", t=NT, s=2),
                               AX.X).then_inc(sem("free6"), 1)

            per_tile = [P, NT, E]
            logit, active, fb, rank, raw, scaled = (rt[:, n, :, :] for n in range(6))
            soft, gated, off, ex = active, fb, rank, scaled

            def stepper(at, first):
                n = [first]

                def step(r):
                    r.then_inc(sem("route_step"), 1)
                    n[0] += 1
                    k = n[0]
                    batch_wait(dve, at, "route_step", 15, k, NEXT)
                return step

            def route_mask(at):
                step = stepper(at, 0)
                batch_wait(dve, at, "norm_step", 3, 3, NEXT)
                bank_read(dve, at, ("logits", ()), NEXT)
                step(dve.tensor_tensor(scaled, raw, rnorm[:, 2, :].unsqueeze(2).to_broadcast(per_tile), ALU.mult))
                step(dve.tensor_tensor(logit, scaled, gate_sb[:, 2, :].unsqueeze(1).to_broadcast(per_tile), ALU.subtract))
                step(dve.tensor_scalar(active, logit, 0.0, None, ALU.is_gt))
                step(dve.reduce_max(rv[:, 0, :], active, AX.X))
                quad = [P, NT, E, E]
                above = cmp2[:, 0, :, :].rearrange("p t (e j) -> p t e j", e=E)
                equal = cmp2[:, 1, :, :].rearrange("p t (e j) -> p t e j", e=E)
                theirs, mine = logit.unsqueeze(2).to_broadcast(quad), logit.unsqueeze(3).to_broadcast(quad)
                step(dve.tensor_tensor(above, theirs, mine, ALU.is_gt))
                step(dve.tensor_tensor(equal, theirs, mine, ALU.is_equal))
                step(dve.tensor_tensor(equal, equal, earlier[:, :, :].unsqueeze(1).to_broadcast(quad), ALU.mult))
                step(dve.tensor_tensor(above, above, equal, ALU.add))
                step(dve.reduce_sum(rank, above, AX.X))
                step(dve.tensor_scalar(rv[:, 1, :], rv[:, 0, :], -1.0, 1.0, ALU.mult, ALU.add))
                step(dve.scalar_tensor_tensor(fb, rank, 2.0, rv[:, 1, :].unsqueeze(2).to_broadcast(per_tile), ALU.is_lt, ALU.mult))
                dve.tensor_tensor(maskb, active, fb, ALU.max).then_inc(sem("mask_ready"), 1)

            def mask_turn(at):
                bank_full(dve, at, ("mask_turn", ()))
                batch_wait(dve, at, "mask_stored", 16, 0, NEXT)
                dve.tensor_copy(maskt[:, :], banks[3].bitcast(bf16)[0:E * NT, 0:P]).then_inc(sem("mask_turned"), 1)

            def route_max(at):
                step = stepper(at, 11)
                batch_wait(dve, at, "mask_ready", 1, 1, NEXT)
                step(dve.tensor_scalar(gated, logit, 0.0, None, ALU.max))
                step(dve.tensor_scalar(off, maskb, OFF, -OFF, ALU.mult, ALU.add))
                step(dve.tensor_tensor(raw, off, gated, ALU.add))
                step(dve.reduce_max(rv[:, 2, :], raw, AX.X))
                dve.tensor_tensor(ex, raw, rv[:, 2, :].unsqueeze(2).to_broadcast(per_tile),
                                  ALU.subtract).then_inc(sem("route_shifted"), 1)

            def route_soft(at):
                par = (at.k0 + NEXT) % 2
                batch_wait(dve, at, "route_exp", 1, 1, NEXT)
                dve.reduce_sum(rv[:, 3, :], ex, AX.X).then_inc(sem("soft_step"), 1)
                batch_wait(dve, at, "soft_step", 3, 1, NEXT)
                dve.reciprocal(rv[:, 4, :], rv[:, 3, :]).then_inc(sem("soft_step"), 1)
                batch_wait(dve, at, "soft_step", 3, 2, NEXT)
                dve.tensor_tensor(soft, ex, rv[:, 4, :].unsqueeze(2).to_broadcast(per_tile),
                                  ALU.mult).then_inc(sem("soft_step"), 1)
                batch_wait(dve, at, "soft_step", 3, 3, NEXT)
                dve.tensor_tensor(gw[:, par, :, :], soft, maskb, ALU.mult).then_inc(sem("gw_ready"), 1)

            def mask(at, u):
                h, e = divmod(u, E)
                who = BATCH["mask", (u,)]
                par = (at.k0 + who) % 2
                n, slot = u // 2, u // 2 % MK_RING
                if at.k0 + who == 0 and u < XM_RING:
                    dve.wait_ge(sem("qkv_split"), u // 2 + 1)
                batch_wait(dve, at, f"mask_loaded{slot}", 32, 16 * (n // MK_RING + 1), who)
                old = u - XM_RING
                if old % E == E - 1:
                    batch_wait(dve, at, "acc_full", 6, 3 * (old // E) + 3, who)
                else:
                    done = lambda k: k // E * (E - 1) + k % E + 1
                    batch_wait(dve, at, "xm_used", 2 * (E - 1), done(old), who)
                dve.tensor_tensor(xm[:, u % XM_RING, :, :], x1t[:, par, :, h * HT:(h + 1) * HT],
                                  mk[:, slot, u % 2, :].unsqueeze(1).to_broadcast([P, 2 * KC, HT]),
                                  ALU.mult).then_inc(sem("xm_ready"), 1)

            def qkv_out(at, h, o):
                if o == 2:
                    return
                tok = slice(h * HT, (h + 1) * HT)
                batch_wait(dve, at, "qk_high", 4, 2 * h + o + 1, THIS)
                dve.scalar_tensor_tensor(qk[:, 1, o, tok], banks[o], QK_SCALE[o], qk[:, 0, o, tok].bitcast(f32),
                                         ALU.mult, ALU.subtract).then_inc(sem("qk_split"), 1)

            def v_turn(at, h):
                who = BATCH["v_turn", (h,)]
                batch_wait(dve, at, "vh_ready", 2, h + 1, who)
                dve.tensor_tensor(v[:, 1, 4 * h:4 * h + 4, :].rearrange("p n d -> p (n d)"), bank_of(at, ("v_turn", (h,))),
                                  v[:, 0, 4 * h:4 * h + 4, :].rearrange("p n d -> p (n d)"), ALU.subtract).then_inc(free_signal(at, ("v_turn", (h,))), 1)

            def score(at, j):
                who = BATCH["score", (j,)]
                w = (j + 1) * P
                bank_full(dve, at, ("score", (j,)))
                src = bank_of(at, ("score", (j,)))[:, 0:w]
                dve.reduce_max(negmax[:, j:j + 1], src, AX.X, negate=True).then_inc(sem("max_found"), 1)

            def p_turn(at, j, part):
                who = BATCH["p_turn", (j, part)]
                n = min(4, j + 1 - 4 * part)
                k = j + 1 if j < 4 else 4 + 2 * (j - 4) + part + 1
                batch_wait(dve, at, "pth_ready", 12, k, who)
                dst = (slice(None), slice(4 * part, 4 * part + n), slice((j % 4) * P, (j % 4 + 1) * P))
                src = bank_of(at, ("p_turn", (j, part)))[:, 0:n * P].rearrange("p (n q) -> p n q", n=n)
                dve.tensor_tensor(pt[:, 1, dst[1], dst[2]], src, pt[:, 0, dst[1], dst[2]],
                                  ALU.subtract).then_inc(free_signal(at, ("p_turn", (j, part))), 1)

            def pv(at, c):
                who = BATCH["pv", (c,)]
                batch_wait(dve, at, "ah_ready", 2, c + 1, who)
                dve.tensor_tensor(a[:, 1, :], bank_of(at, ("pv", (c,))), a[:, 0, :].bitcast(f32),
                                  ALU.subtract).then_inc(free_signal(at, ("pv", (c,))), 1)

            def weigh(at, c):
                who = BATCH["weigh", (c,)]
                par = (at.k0 + who) % 2
                t4 = slice(4 * c, 4 * c + 4)
                bank_read(dve, at, ("score", (4 * c + 3,)), who)
                batch_wait(dve, at, "gw_ready", 1, 1, who)
                dve.reciprocal(pinv[:, t4], psums[:, t4]).then_inc(sem("sum_inverted"), 1)
                batch_wait(dve, at, "sum_inverted", 2, c + 1, who)
                dve.tensor_tensor(cw[:, t4, :], gw[:, par, t4, :], pinv[:, t4].unsqueeze(2).to_broadcast([P, 4, E]),
                                  ALU.mult).then_inc(sem("weighed"), 1)

            def o_proj_part(at, j, part):
                if part % 2:
                    return
                who = BATCH["o_proj", (j, part)]
                par = (at.k0 + who) % 2
                batch_wait(dve, at, "weighed", 2, j // 4 + 1, who)
                bank_full(dve, at, ("o_proj", (j, part)))
                for i in range(2):
                    batch_wait(dve, at, "main_added", 4 * NT, 4 * j + part + i, who)
                    dve.scalar_tensor_tensor(x1[:, par, j, :], bank_of(at, ("o_proj", (j, part)))[:, i * C:(i + 1) * C],
                                             cw[:, j, 2 * part + i:2 * part + i + 1], x1[:, par, j, :],
                                             ALU.mult, ALU.add).then_inc(sem("main_added"), 1)

            def tile_end(at, j):
                who = BATCH["tile_end", (j,)]
                par = (at.k0 + who) % 2
                batch_wait(dve, at, "main_added", 4 * NT, 4 * j + 4, who)
                batch_wait(dve, at, "side_added", 3 * NT, 3 * j + 3, who)
                if j % 4 == 0:
                    batch_wait(dve, at, "y_free", 2 * 16, 16 * (j // 4 + 1), who)
                dve.tensor_tensor(y[:, j % 4, :], x1[:, par, j, :], side[:, j % 2, :], ALU.add).then_inc(sem("tile_summed"), 1)
                batch_wait(dve, at, "tile_summed", NT, j + 1, who)
                dve.bn_stats(st2[:, j, :], y[:, j % 4, :]).then_inc(sem("fin_partial"), 1)
                alone(dve)
                batch_wait(dve, at, "fin_partial", NT, j + 1, who)
                dve.bn_aggr(mv2[:, j, :], st2[:, j, :]).then_inc(sem("fin_stats"), 1)

            def fin_norm(at, c):
                t4 = slice(4 * c, 4 * c + 4)
                batch_wait(dve, at, "fin_rstd", 2, c + 1, PREV)
                dve.scalar_tensor_tensor(shift2[:, t4], mv2[:, t4, 0], -1.0, rs2[:, t4], ALU.mult,
                                         ALU.mult).then_inc(sem("fin_shift"), 1)

            walk(dve, {"x_turn": x_turn, "inp": inp, "h_split": h_split, "x1_sum": x1_sum, "ln": ln, "ln_shift": ln_shift,
                       "norm_root": norm_root, "x1_turn": x1_turn, "logits": logits, "route_mask": route_mask, "mask_turn": mask_turn, "route_max": route_max,
                       "route_soft": route_soft, "mask": mask, "qkv_out": qkv_out, "v_turn": v_turn, "score": score,
                       "p_turn": p_turn, "pv": pv, "weigh": weigh, "o_proj": o_proj_part, "tile_end": tile_end,
                       "fin_norm": fin_norm, "w_low": w_low, "biases": biases, "sim_sum": sim_sum,
                       "sim_norm": sim_norm})

        @block.gpsimd
        def _(pool):
            pool.memset(ident[:, :], 0.0).then_inc(sem("cleared"), 1)
            pool.memset(causal[:, :], 0.0).then_inc(sem("cleared"), 1)
            pool.memset(earlier[:, :, :], 1.0).then_inc(sem("cleared"), 1)
            pool.memset(halves[:, 0:NT], -0.5).then_inc(sem("cleared"), 1)
            pool.memset(halves[:, NT:2 * NT], 0.5).then_inc(sem("cleared"), 1)
            pool.memset(ones, 1.0).then_inc(sem("cleared"), 1)
            pool.memset(epsilons[:, :], EPS).then_inc(sem("cleared"), 1)
            pool.memset(channels[:, :], float(C)).then_inc(sem("cleared"), 1)
            pool.memset(maskb2[:, 1, :, :], 0.0).then_inc(sem("cleared"), 1)
            pool.wait_ge(sem("cleared"), 9)
            pool.affine_select(out=ident[:, :], in_=ident[:, :], compare_op=ALU.not_equal, fill=1.0, base=0,
                               pattern=[[-1, P]], channel_multiplier=1).then_inc(sem("selected"), 1)
            pool.wait_ge(sem("selected"), 1)
            pool.tensor_copy(identb[:, :], ident[:, :]).then_inc(sem("consts"), 1)
            pool.affine_select(out=causal[:, :], in_=causal[:, :], compare_op=ALU.is_ge, fill=CAUSAL, base=0,
                               pattern=[[-1, P]], channel_multiplier=1).then_inc(sem("masks_made"), 1)
            pool.affine_select(out=earlier[:, :, :], in_=earlier[:, :, :], compare_op=ALU.is_gt, fill=0.0, base=0,
                               pattern=[[1, E], [-1, E]], channel_multiplier=0).then_inc(sem("masks_made"), 1)

            def sim_sum(at):
                pool.wait_ge(sem("sim_sum_copied"), 1)
                pool.tensor_tensor(sim_n[:, 1, :], sim_n[:, 0, :], halves[:, NT:NT + E], ALU.pow).then_inc(sem("sim_rooted"), 1)

            def x_turn(at, g):
                if g < 3:
                    return
                if at.k0 == -1:
                    pool.wait_ge(sem("small_loaded"), 80)
                for k in (0, 2, 3):
                    bank_full(pool, at, ("x_turn", (k,)))
                pool.tensor_tensor(xin[:, :, :], xin[:, :, :], bias_o[:, :].unsqueeze(1).to_broadcast([P, NT, C]),
                                   ALU.add).then_inc(sem("xb_ready"), 1)

            def ln(at, c):
                t4 = slice(4 * c, 4 * c + 4)
                batch_wait(pool, at, "ln_stats", 2, c + 1, NEXT)
                pool.tensor_tensor(vp[:, t4], mv[:, t4, 1], epsilons[:, t4], ALU.add).then_inc(sem("ln_var"), 1)
                batch_wait(pool, at, "ln_var", 3, c + 1, NEXT)
                pool.tensor_tensor(rs[:, t4], vp[:, t4], halves[:, t4], ALU.pow).then_inc(sem("ln_rstd"), 1)

            def norm_root(at):
                pool.tensor_tensor(vp[:, NT:2 * NT], mv[:, :, 1], channels[:, :], ALU.mult).then_inc(sem("ln_var"), 1)
                batch_wait(pool, at, "ln_var", 3, 3, NEXT)
                pool.tensor_tensor(rs[:, NT:2 * NT], vp[:, NT:2 * NT], halves[:, NT:2 * NT], ALU.pow).then_inc(sem("norm_rooted"), 1)

            def o_proj_part(at, j, part):
                if part % 2 == 0:
                    return
                who = BATCH["o_proj", (j, part)]
                for i in range(part == 1, 2):
                    n = 3 * j + part - 2 + i
                    batch_wait(pool, at, "side_scaled", 4 * NT, 4 * j + part + i, who)
                    if n % 3:
                        batch_wait(pool, at, "side_added", 3 * NT, n, who)
                    pool.tensor_tensor(side[:, j % 2, :], side[:, j % 2, :], tmp[:, n % TMP_RING, :],
                                       ALU.add).then_inc(sem("side_added"), 1)

            def fin(at, c):
                t4 = slice(4 * c, 4 * c + 4)
                batch_wait(pool, at, "fin_stats", NT, 4 * c + 4, PREV)
                pool.tensor_tensor(vp2[:, t4], mv2[:, t4, 1], epsilons[:, t4], ALU.add).then_inc(sem("fin_var"), 1)
                batch_wait(pool, at, "fin_var", 2, c + 1, PREV)
                pool.tensor_tensor(rs2[:, t4], vp2[:, t4], halves[:, 0:4], ALU.pow).then_inc(sem("fin_rstd"), 1)

            walk(pool, {"sim_sum": sim_sum, "x_turn": x_turn, "ln": ln, "norm_root": norm_root, "o_proj": o_proj_part, "fin": fin})


_INS = ["L0_attn_x", "L0_attn_Wi", "L0_attn_bi", "L0_attn_Wg", "L0_attn_bg", "L0_attn_Wo", "L0_attn_bo",
        "L0_ffn_sim_matrix", "L0_ffn_gates", "L0_ffn_q_proj", "L0_ffn_k_proj", "L0_ffn_v_proj", "L0_ffn_o_proj"]
_OUTS = [((B, T, C), "float32")]


def kernel(**inputs):
    import concourse.bacc as _bacc
    from concourse.bass_utils import run_bass_kernel_spmd as _run

    nc = _bacc.Bacc("TRN2", target_bir_lowering=False, num_devices=1)
    arrays, args = {}, []
    for name in _INS:
        arr = np.ascontiguousarray(inputs[name])
        arrays[f"in_{name}_dram"] = arr
        args.append(nc.dram_tensor(f"in_{name}_dram", arr.shape, mybir.dt.from_np(arr.dtype), kind="ExternalInput").ap())
    for i, (shape, dtype) in enumerate(_OUTS):
        args.append(nc.dram_tensor(f"out_{i}_dram", shape, mybir.dt.from_np(np.dtype(dtype)), kind="ExternalOutput").ap())
    rglru_moe(nc, *args)
    r = _run(nc, [arrays], core_ids=[0])
    return r.results[0]["out_0_dram"]
```
